# Optimizing a Trainium2 kernel written in Bass

```python
import numpy as np
import jax
import jax.numpy as jnp

def _softmax(x, axis=-1):
    return jax.nn.softmax(x, axis=axis)

def _gelu(x):
    return jax.nn.gelu(x, approximate=True)

def _silu(x):
    return jax.nn.silu(x)

def _sigmoid(x):
    return jax.nn.sigmoid(x)

def _layernorm(x, axis=-1, eps=1e-05):
    m = jnp.mean(x, axis=axis, keepdims=True)
    v = jnp.var(x, axis=axis, keepdims=True)
    return (x - m) / jnp.sqrt(v + eps)

def _scatter_add(tgt, idx, src, axis=0):
    return tgt.at[idx].add(src)

def _segment_sum(src, seg, n):
    return jax.ops.segment_sum(src, seg, n)
kernel_name = 'mk_prb_d1_jaxref_r8_a50ee6'

def setup_inputs(seed: int=0):
    np.random.seed(seed)
    _w = jnp.asarray

    def _L0_attn_setup():
        import jax, jax.numpy as jnp
        import numpy as np
        D_MODEL = 128
        N_HEADS = 16
        WINDOW = 32
        S_DIM = 128
        BATCH = 1
        SEQ = 512
        EPS = 1e-05

        def _layernorm(x, g, b):
            mu = jnp.mean(x, -1, keepdims=True)
            var = jnp.mean((x - mu) ** 2, -1, keepdims=True)
            return (x - mu) * jax.lax.rsqrt(var + EPS) * g + b

        def _windowed_attn(xn, W_qkv, W_O, b_O):
            Bq, T, d = xn.shape
            H, Dh, C = (N_HEADS, d // N_HEADS, WINDOW)
            N = T // C
            qkv = xn @ W_qkv
            q, k, v = jnp.split(qkv, 3, axis=-1)

            def blk(t):
                return t.reshape(Bq, T, H, Dh).transpose(0, 2, 1, 3).reshape(Bq, H, N, C, Dh)
            Qb, Kb, Vb = (blk(q), blk(k), blk(v))

            def win(t):
                prev = jnp.concatenate([jnp.zeros_like(t[:, :, :1]), t[:, :, :-1]], axis=2)
                return jnp.concatenate([prev, t], axis=3)
            Kw, Vw = (win(Kb), win(Vb))
            scores = jnp.einsum('bhncd,bhnkd->bhnck', Qb, Kw) / np.sqrt(Dh).astype(np.float32)
            qi = jnp.arange(C)[:, None]
            kk = jnp.arange(2 * C)[None, :]
            band = (kk > qi) & (kk <= qi + C)
            mask = jnp.where((jnp.arange(N) == 0)[:, None, None], band & (kk >= C), band)
            scores = jnp.where(mask[None, None], scores, -jnp.inf)
            p = jax.nn.softmax(scores, axis=-1)
            o = jnp.einsum('bhnck,bhnkd->bhncd', p, Vw)
            o = o.reshape(Bq, H, T, Dh).transpose(0, 2, 1, 3).reshape(Bq, T, d)
            return o @ W_O + b_O
        key = jax.random.key(seed)
        ks = jax.random.split(key, 10)
        d, s = (D_MODEL, S_DIM)

        def w(k, shape, fan_in):
            return jax.random.normal(k, shape, jnp.float32) * fan_in ** (-0.5)
        return {'x': jax.random.normal(ks[0], (BATCH, SEQ, d), jnp.float32), 'ln1_g': jnp.ones((d,), jnp.float32), 'ln1_b': jnp.zeros((d,), jnp.float32), 'ln2_g': jnp.ones((d,), jnp.float32), 'ln2_b': jnp.zeros((d,), jnp.float32), 'W_qkv': w(ks[1], (d, 3 * d), d), 'W_O': w(ks[2], (d, d), d), 'b_O': jnp.zeros((d,), jnp.float32), 'W_ug': w(ks[3], (d, s + d), d), 'b_ug': jnp.zeros((s + d,), jnp.float32), 'B_w': w(ks[4], (d, s), d), 'A': jax.random.uniform(ks[5], (s,), jnp.float32, -0.1, 0.1), 'C_w': w(ks[6], (s, d), s), 'mlp_W1': w(ks[7], (d, 4 * d), d), 'mlp_b1': jnp.zeros((4 * d,), jnp.float32), 'mlp_W2': w(ks[8], (4 * d, d), 4 * d), 'mlp_b2': jnp.zeros((d,), jnp.float32)}
    _L0_attn_in = _L0_attn_setup()

    def _L0_ffn_setup():
        import jax, jax.numpy as jnp
        import numpy as np
        EPS = 1e-05

        def _ln_stats(x):
            mu = jnp.mean(x, axis=-1, keepdims=True)
            var = jnp.mean((x - mu) ** 2, axis=-1, keepdims=True)
            return (x - mu) * jax.lax.rsqrt(var + EPS)
        B, S, H, I, E = (2, 256, 128, 512, 8)
        key = jax.random.key(seed)
        ks = jax.random.split(key, 8)
        inp = {'hidden_states': jax.random.normal(ks[0], (B, S, H), dtype=jnp.float32), 'router_ln_w': jnp.ones((H,), jnp.float32), 'router_ln_b': jnp.zeros((H,), jnp.float32), 'router_w': jax.random.normal(ks[1], (H, E), dtype=jnp.float32) * 0.02, 'router_b': jnp.zeros((E,), jnp.float32), 'exp_ln_w': jnp.ones((E, H), jnp.float32), 'exp_ln_b': jnp.zeros((E, H), jnp.float32), 'w1': jax.random.normal(ks[2], (E, H, I), dtype=jnp.float32) * 0.02, 'b1': jnp.zeros((E, I), jnp.float32), 'w2': jax.random.normal(ks[3], (E, I, H), dtype=jnp.float32) * 0.02, 'b2': jnp.zeros((E, H), jnp.float32), 'out_ln_w': jnp.ones((H,), jnp.float32), 'out_ln_b': jnp.zeros((H,), jnp.float32)}
        return inp
    _L0_ffn_in = _L0_ffn_setup()
    _d = {'L0_attn_x': _L0_attn_in['x'], 'L0_attn_ln1_g': _L0_attn_in['ln1_g'], 'L0_attn_ln1_b': _L0_attn_in['ln1_b'], 'L0_attn_ln2_g': _L0_attn_in['ln2_g'], 'L0_attn_ln2_b': _L0_attn_in['ln2_b'], 'L0_attn_W_qkv': _L0_attn_in['W_qkv'], 'L0_attn_W_O': _L0_attn_in['W_O'], 'L0_attn_b_O': _L0_attn_in['b_O'], 'L0_attn_W_ug': _L0_attn_in['W_ug'], 'L0_attn_b_ug': _L0_attn_in['b_ug'], 'L0_attn_B_w': _L0_attn_in['B_w'], 'L0_attn_A': _L0_attn_in['A'], 'L0_attn_C_w': _L0_attn_in['C_w'], 'L0_attn_mlp_W1': _L0_attn_in['mlp_W1'], 'L0_attn_mlp_b1': _L0_attn_in['mlp_b1'], 'L0_attn_mlp_W2': _L0_attn_in['mlp_W2'], 'L0_attn_mlp_b2': _L0_attn_in['mlp_b2'], 'L0_ffn_router_ln_w': _L0_ffn_in['router_ln_w'], 'L0_ffn_router_ln_b': _L0_ffn_in['router_ln_b'], 'L0_ffn_router_w': _L0_ffn_in['router_w'], 'L0_ffn_router_b': _L0_ffn_in['router_b'], 'L0_ffn_exp_ln_w': _L0_ffn_in['exp_ln_w'], 'L0_ffn_exp_ln_b': _L0_ffn_in['exp_ln_b'], 'L0_ffn_w1': _L0_ffn_in['w1'], 'L0_ffn_b1': _L0_ffn_in['b1'], 'L0_ffn_w2': _L0_ffn_in['w2'], 'L0_ffn_b2': _L0_ffn_in['b2'], 'L0_ffn_out_ln_w': _L0_ffn_in['out_ln_w'], 'L0_ffn_out_ln_b': _L0_ffn_in['out_ln_b']}
    _x0 = _d['L0_attn_x']
    _d['L0_attn_x'] = jax.random.normal(jax.random.fold_in(jax.random.key(seed), 1), (4, 512, 128), dtype=_x0.dtype)
    del _x0
    return _d

def reference(L0_attn_x, L0_attn_ln1_g, L0_attn_ln1_b, L0_attn_ln2_g, L0_attn_ln2_b, L0_attn_W_qkv, L0_attn_W_O, L0_attn_b_O, L0_attn_W_ug, L0_attn_b_ug, L0_attn_B_w, L0_attn_A, L0_attn_C_w, L0_attn_mlp_W1, L0_attn_mlp_b1, L0_attn_mlp_W2, L0_attn_mlp_b2, L0_ffn_router_ln_w, L0_ffn_router_ln_b, L0_ffn_router_w, L0_ffn_router_b, L0_ffn_exp_ln_w, L0_ffn_exp_ln_b, L0_ffn_w1, L0_ffn_b1, L0_ffn_w2, L0_ffn_b2, L0_ffn_out_ln_w, L0_ffn_out_ln_b):

    def _L0_attn_ref(x, ln1_g, ln1_b, ln2_g, ln2_b, W_qkv, W_O, b_O, W_ug, b_ug, B_w, A, C_w, mlp_W1, mlp_b1, mlp_W2, mlp_b2):
        import jax, jax.numpy as jnp
        import numpy as np
        D_MODEL = 128
        N_HEADS = 16
        WINDOW = 32
        S_DIM = 128
        BATCH = 1
        SEQ = 512
        EPS = 1e-05

        def _layernorm(x, g, b):
            mu = jnp.mean(x, -1, keepdims=True)
            var = jnp.mean((x - mu) ** 2, -1, keepdims=True)
            return (x - mu) * jax.lax.rsqrt(var + EPS) * g + b

        def _windowed_attn(xn, W_qkv, W_O, b_O):
            Bq, T, d = xn.shape
            H, Dh, C = (N_HEADS, d // N_HEADS, WINDOW)
            N = T // C
            qkv = xn @ W_qkv
            q, k, v = jnp.split(qkv, 3, axis=-1)

            def blk(t):
                return t.reshape(Bq, T, H, Dh).transpose(0, 2, 1, 3).reshape(Bq, H, N, C, Dh)
            Qb, Kb, Vb = (blk(q), blk(k), blk(v))

            def win(t):
                prev = jnp.concatenate([jnp.zeros_like(t[:, :, :1]), t[:, :, :-1]], axis=2)
                return jnp.concatenate([prev, t], axis=3)
            Kw, Vw = (win(Kb), win(Vb))
            scores = jnp.einsum('bhncd,bhnkd->bhnck', Qb, Kw) / np.sqrt(Dh).astype(np.float32)
            qi = jnp.arange(C)[:, None]
            kk = jnp.arange(2 * C)[None, :]
            band = (kk > qi) & (kk <= qi + C)
            mask = jnp.where((jnp.arange(N) == 0)[:, None, None], band & (kk >= C), band)
            scores = jnp.where(mask[None, None], scores, -jnp.inf)
            p = jax.nn.softmax(scores, axis=-1)
            o = jnp.einsum('bhnck,bhnkd->bhncd', p, Vw)
            o = o.reshape(Bq, H, T, Dh).transpose(0, 2, 1, 3).reshape(Bq, T, d)
            return o @ W_O + b_O
        xn = _layernorm(x, ln1_g, ln1_b)
        attn = _windowed_attn(xn, W_qkv, W_O, b_O)
        ug = xn @ W_ug + b_ug
        u = ug[..., :S_DIM]
        g = jax.nn.sigmoid(ug[..., S_DIM:])
        drive = xn @ B_w + u

        def step(s, ut):
            s2 = A * s + ut
            return (s2, s2)
        s0 = jnp.zeros((x.shape[0], S_DIM), x.dtype)
        _, states = jax.lax.scan(step, s0, drive.transpose(1, 0, 2))
        y_ssm = jnp.einsum('tbs,sd->btd', states, C_w)
        x = x + g * attn + (1.0 - g) * y_ssm
        h = _layernorm(x, ln2_g, ln2_b)
        x = x + jax.nn.gelu(h @ mlp_W1 + mlp_b1, approximate=False) @ mlp_W2 + mlp_b2
        return x

    def _L0_ffn_ref(hidden_states, router_ln_w, router_ln_b, router_w, router_b, exp_ln_w, exp_ln_b, w1, b1, w2, b2, out_ln_w, out_ln_b):
        import jax, jax.numpy as jnp
        import numpy as np
        EPS = 1e-05

        def _ln_stats(x):
            mu = jnp.mean(x, axis=-1, keepdims=True)
            var = jnp.mean((x - mu) ** 2, axis=-1, keepdims=True)
            return (x - mu) * jax.lax.rsqrt(var + EPS)
        K = 2
        x = hidden_states
        xhat = _ln_stats(x)
        router_logits = (xhat * router_ln_w + router_ln_b) @ router_w + router_b
        routing_weights, selected = jax.lax.top_k(router_logits, K)
        routing_weights = jax.nn.softmax(routing_weights, axis=-1)
        xn = xhat[None] * exp_ln_w[:, None, None, :] + exp_ln_b[:, None, None, :]
        h = jnp.einsum('ebsh,ehi->ebsi', xn, w1) + b1[:, None, None, :]
        h = jax.nn.gelu(h, approximate=False)
        eo = jnp.einsum('ebsi,eih->ebsh', h, w2) + b2[:, None, None, :]
        eo = jnp.moveaxis(eo, 0, 2)
        gathered = jnp.take_along_axis(eo, selected[..., None], axis=2)
        combined = jnp.sum(routing_weights[..., None] * gathered, axis=2)
        return _ln_stats(combined) * out_ln_w + out_ln_b
    x = L0_attn_x
    xn = _layernorm(x, axis=-1)
    x = x + _L0_attn_ref(xn, L0_attn_ln1_g, L0_attn_ln1_b, L0_attn_ln2_g, L0_attn_ln2_b, L0_attn_W_qkv, L0_attn_W_O, L0_attn_b_O, L0_attn_W_ug, L0_attn_b_ug, L0_attn_B_w, L0_attn_A, L0_attn_C_w, L0_attn_mlp_W1, L0_attn_mlp_b1, L0_attn_mlp_W2, L0_attn_mlp_b2) + _L0_ffn_ref(xn, L0_ffn_router_ln_w, L0_ffn_router_ln_b, L0_ffn_router_w, L0_ffn_router_b, L0_ffn_exp_ln_w, L0_ffn_exp_ln_b, L0_ffn_w1, L0_ffn_b1, L0_ffn_w2, L0_ffn_b2, L0_ffn_out_ln_w, L0_ffn_out_ln_b)
    return x

_drawn_inputs = setup_inputs


def setup_inputs(seed=0):
    import zlib

    import numpy as np

    out = dict(_drawn_inputs(seed))
    spreads = {'L0_attn_ln1_g': (1.0, 0.2),
     'L0_attn_ln1_b': (0.0, 0.1),
     'L0_attn_ln2_g': (1.0, 0.2),
     'L0_attn_ln2_b': (0.0, 0.281),
     'L0_attn_b_O': (0.0, 0.309),
     'L0_attn_b_ug': (0.0, 0.299),
     'L0_attn_mlp_b1': (0.0, 0.293),
     'L0_attn_mlp_b2': (0.0, 0.1),
     'L0_ffn_router_ln_w': (1.0, 0.2),
     'L0_ffn_router_ln_b': (0.0, 0.1),
     'L0_ffn_router_b': (0.0, 0.1),
     'L0_ffn_exp_ln_w': (1.0, 0.2),
     'L0_ffn_exp_ln_b': (0.0, 0.402),
     'L0_ffn_b1': (0.0, 0.1),
     'L0_ffn_b2': (0.0, 0.1),
     'L0_ffn_out_ln_w': (1.0, 0.2),
     'L0_ffn_out_ln_b': (0.0, 0.1)}
    factors = {}
    for name, (base, spread) in spreads.items():
        noise = np.random.default_rng([zlib.crc32(name.encode()), seed]).standard_normal(out[name].shape)
        drawn = base * np.exp(spread * noise) if base else spread * noise
        out[name] = jnp.asarray(drawn.astype(out[name].dtype))
    for name, factor in factors.items():
        out[name] = (out[name] * factor).astype(out[name].dtype)
    return out
```

```python
from contextlib import ExitStack

import numpy as np

import concourse.bass as bass
from concourse import mybir

ALU = mybir.AluOpType
ACT = mybir.ActivationFunctionType
F32 = mybir.dt.float32
BF16 = mybir.dt.bfloat16
I32 = mybir.dt.int32
U32 = mybir.dt.uint32
AX_X = mybir.AxisListType.X

P = 128
D = 128
NB, SEQ = 4, 512
T = NB * SEQ // P
TB = SEQ // P
H, DH = 16, 8
HG = 4
W = 32
NBLK = SEQ // W
NCH = NBLK // 2
E, FF, K = 8, 512, 2
FC = FF // P
NT = (NB * SEQ * K) // P + E - 1
MB = NB * SEQ // P
EPS = 1e-5
NEG = -1e30

C_ID = 0
C_TRI = C_ID + P
C_HEAD = C_TRI + P
C_BLK = C_HEAD + H
C_MASK = C_BLK + W
C_RESET = C_MASK + 4 * W
C_IE = C_RESET + E * T
C_J = C_IE + E
C_TI = C_J + MB
C_SEL = C_TI + NT
C_N = C_SEL + E
V_G1, V_B1, V_G2, V_B2, V_BU, V_A, V_RW, V_RB = range(8)
V_M1 = 8
V_EW = V_M1 + FC
V_EB = V_EW + E
V_N = V_EB + E
R_G, R_O, R_M2, R_E1, R_E2 = 0, D, 2 * D, 3 * D, 3 * D + FF
R_N = R_E2 + D
QR = 32
RP = 3 * QR


def constants():
    c = np.zeros((P, C_N), np.float32)
    p = np.arange(P)
    c[:, C_ID:C_ID + P] = np.eye(P)
    c[:, C_TRI:C_TRI + P] = p[:, None] < p[None, :]
    c[:, C_HEAD:C_HEAD + H] = p[:, None] // DH == np.arange(H)[None, :]
    c[:, C_BLK:C_BLK + W] = p[:, None] // W == np.arange(W)[None, :] // DH
    q, k = p[:, None] % W, np.arange(2 * W)[None, :]
    band = (k > q) & (k <= q + W)
    c[:, C_MASK:C_MASK + 2 * W] = np.where(band & (k >= W), 0.0, NEG)
    c[:, C_MASK + 2 * W:C_MASK + 4 * W] = np.where(band, 0.0, NEG)
    c[:, C_RESET:C_RESET + E * T] = np.arange(E * T)[None, :] % T != 0
    c[:, C_IE:C_IE + E] = np.arange(E)
    c[:, C_J:C_J + MB] = np.arange(MB) * P
    c[:, C_TI:C_TI + NT] = np.arange(NT)
    c[:, C_SEL:C_SEL + E] = p[:, None] % QR == np.arange(E)[None, :]
    return c


def program(nc, x_d, const_d, vec_d, row_d, wqkv_d, wo_d, wug_d, bw_d, cw_d, m1_d, m2_d,
            rw_d, rb_d, w1_d, w2_d, ow_d, ob_d, out_d):
    xs_d = nc.dram_tensor("sorted_rows", (NT * P, D), F32).ap()
    es_d = nc.dram_tensor("expert_rows", (NT * P, D), F32).ap()
    mm = nc.tensor.matmul
    ctx = ExitStack()
    with ctx:
        def sb(name, shape, dt=F32):
            return ctx.enter_context(nc.sbuf_tensor(name, shape, dt))

        def bank(name):
            return ctx.enter_context(nc.psum_tensor(name, [P, 512], F32))

        def sem(name):
            return ctx.enter_context(nc.semaphore(name))

        const = sb("const", [P, C_N])
        vec = sb("vec", [P, V_N])
        rowf = sb("rowf", [RP, R_N])
        rowp = sb("rowp", [RP, R_N], BF16)
        sel0 = sb("sel0", [RP, P], BF16)
        sel = sb("sel", [RP, 2, 2, P], BF16)
        wqkv = sb("wqkv", [P, 3 * D])
        wo = sb("wo", [P, D])
        wug = sb("wug", [P, 2 * D])
        bw = sb("bw", [P, D])
        cw = sb("cw", [P, D])
        m1 = sb("m1", [P, FF])
        m2 = sb("m2", [P, FC, D])
        rw = sb("rw", [P, E])
        rb = sb("rb", [P, E])
        w1 = sb("w1", [P, E, FF])
        w2 = sb("w2", [P, E, FC, D])
        ow = sb("ow", [P, D])
        ob = sb("ob", [P, D])
        wdrive = sb("wdrive", [P, D])
        identb = sb("identb", [P, P], BF16)
        maskb = sb("maskb", [P, 4 * W], BF16)
        ones = sb("ones", [P, P])
        zeros = sb("zeros", [P, D])
        half = sb("half", [P, T])
        ident = const[:, C_ID:C_ID + P]

        x = sb("x", [P, T, D])
        xn = sb("xn", [P, T, D])
        xhat = sb("xhat", [P, T, D])
        xn1T = sb("xn1T", [P, T * P])
        acc = xhat

        st = sb("st", [P, T, 6])
        lnt = sb("lnt", [P, 8, T])
        logit = sb("logit", [P, T, E])
        top = sb("top", [P, T, 8])
        topi = sb("topi", [P, T, 8], U32)
        topf = sb("topf", [P, K, T])
        gw = sb("gw", [P, 4, T])
        pick = sb("pick", [P, K, E, T])
        picks = sb("picks", [P, E * T])
        tot = sb("tot", [P, E * T])
        incl = sb("incl", [P, E * T])
        cmpj = sb("cmpj", [P, E, MB])
        blocks = sb("blocks", [P, 4, E])
        base = sb("base", [P, E * T])
        slotf = sb("slotf", [P, K, E, T])
        slots = sb("slots", [P, K, T])
        sloti = sb("sloti", [P, K, T], I32)
        tcmp = sb("tcmp", [1, NT, E])
        texpf = sb("texpf", [1, 2, NT])
        texp = sb("texp", [1, NT], I32)

        xa = sb("xa", [P, SEQ])
        qT = sb("qT", [P, SEQ])
        kT = sb("kT", [P, SEQ])
        kx = sb("kx", [P, 4, HG, W + SEQ])
        vx = sb("vx", [P, NBLK, D])
        drive = sb("drive", [P, SEQ])
        states = sb("states", [P, SEQ])
        gate = sb("gate", [P, SEQ])
        smax = sb("smax", [P, 2, 8])
        sc = sb("sc", [P, 2, 512])
        pr = sb("pr", [P, 2, 512])
        xrT = pr
        pT = sb("pT", [P, NBLK, HG, 2, W])
        rden = sb("rden", [P, SEQ])
        oT = sb("oT", [P, SEQ])
        yS = sb("yS", [P, SEQ])
        mix = sb("mix", [P, 3, SEQ])
        x2 = sb("x2", [P, SEQ])
        st2 = sb("st2", [P, TB, 6])
        ln2 = sb("ln2", [P, 8, TB])
        hh = sb("hh", [P, SEQ])
        hT = sb("hT", [P, SEQ])
        gT = sb("gT", [P, FC, SEQ])

        xg = sb("xg", [P, 2, D])
        xeT = sb("xeT", [P, 2, P])
        spare = vx[:, :, :].rearrange("p a d -> p (a d)").rearrange("p (k a n) -> p k a n", k=2, a=2)
        he, heT = spare[:, 0], spare[:, 1]
        eo = sb("eo", [P, 2, D])

        rowsk = pT[:, :, :, :, :].rearrange("p a g s q -> p (a g s q)").rearrange("p (k t d) -> p k t d", k=K, t=T)
        comb = gT[:, 0:3, :]
        st3 = sb("st3", [P, TB, 6])
        ln3 = sb("ln3", [P, 8, TB])
        outb = sc

        GA, GB, GC = bank("GA"), bank("GB"), bank("GC")
        S = [bank("S0"), bank("S1")]
        OV, DEN, M2 = bank("OV"), bank("DEN"), bank("M2")

        x_in = sem("x_in")
        w_in = sem("w_in")
        wm_in = sem("wm_in")
        we_in = sem("we_in")
        xs_zero = sem("xs_zero")
        zero_set = sem("zero_set")
        scattered = sem("scattered")
        row_in = [sem("row_in0"), sem("row_in1")]
        row_out = [sem("row_out0"), sem("row_out1")]
        gathered = [sem("gathered0"), sem("gathered1")]
        rows_ready = sem("rows_ready")
        stored = sem("stored")
        pool_pow = sem("pool_pow")
        pool_const = sem("pool_const")
        pool_xa = sem("pool_xa")
        dve = sem("dve_chain")
        dve_setup = sem("dve_setup")
        ln_in = sem("ln_in")
        ln_out = sem("ln_out")
        xh_ready = sem("xh_ready")
        pe_xT = sem("pe_xT")
        dve_xT = sem("dve_xT")
        act_xT = sem("act_xT")
        pe_logit = sem("pe_logit")
        diff_ready = sem("diff_ready")
        diff_exp = sem("diff_exp")
        picks_ready = sem("picks_ready")
        pe_rank = sem("pe_rank")
        slots_ready = sem("slots_ready")
        pe_q, pe_k, pe_drive, pe_v, pe_gate = sem("pe_q"), sem("pe_k"), sem("pe_drive"), sem("pe_v"), sem("pe_gate")
        pe_scores, pe_pv, pe_den, pe_y, pe_attn = sem("pe_scores"), sem("pe_pv"), sem("pe_den"), sem("pe_y"), sem("pe_attn")
        pe_hT, pe_mlp1, pe_mlp2 = sem("pe_hT"), sem("pe_mlp1"), sem("pe_mlp2")
        act_q, act_k, act_kx, act_drive, act_gate = sem("act_q"), sem("act_k"), sem("act_kx"), sem("act_drive"), sem("act_gate")
        act_exp, act_y, act_hT, act_gelu = sem("act_exp"), sem("act_y"), sem("act_hT"), sem("act_gelu")
        dve_kx, dve_vx, dve_scan, dve_max = sem("dve_kx"), sem("dve_vx"), sem("dve_scan"), sem("dve_max")
        dve_sub, dve_pT, dve_rden, dve_oT = sem("dve_sub"), sem("dve_pT"), sem("dve_rden"), sem("dve_oT")
        dve_attn, dve_h, dve_acc = sem("dve_attn"), sem("dve_h"), sem("dve_acc")
        var_ready, rstd_ready = sem("var_ready"), sem("rstd_ready")
        pe_xeT, dve_xeT, pe_he, act_he, pe_heT, dve_heT, pe_eo, dve_eo = (
            sem("pe_xeT"), sem("dve_xeT"), sem("pe_he"), sem("act_he"), sem("pe_heT"), sem("dve_heT"),
            sem("pe_eo"), sem("dve_eo"))
        var3_ready, rstd3_ready, out_ready = sem("var3_ready"), sem("rstd3_ready"), sem("out_ready")

        block = ctx.enter_context(nc.Block())

        def tok3(ap):
            return ap.rearrange("p (t d) -> p t d", d=D)

        def chain(eng, count):
            def link(ins):
                count[0] += 1
                ins.then_inc(dve, 1)
                eng.wait_ge(dve, count[0])
            return link

        @block.sync
        def _(sp):
            sp.dma_start(x[:, :, :], x_d.rearrange("b (t p) d -> p (b t) d", p=P)).then_inc(x_in, 16)
            for dst, src in ((const[:, :], const_d), (vec[:, :], vec_d), (rw[:, :], rw_d),
                             (rb[:, :], rb_d.unsqueeze(0).to_broadcast([P, E]))):
                sp.dma_start(dst, src).then_inc(w_in, 16)
            for dst, src in ((wqkv[:, :], wqkv_d), (wug[:, :], wug_d), (bw[:, :], bw_d), (rowf[:, :], row_d),
                             (wo[:, :], wo_d), (cw[:, :], cw_d), (m1[:, :], m1_d),
                             (m2[:, :, :], m2_d.rearrange("(c p) d -> p c d", p=P))):
                sp.dma_start(dst, src).then_inc(wm_in, 16)
            for e in range(E):
                sp.dma_start(w1[:, e, :], w1_d[e]).then_inc(we_in, 16)
                sp.dma_start(w2[:, e, :, :], w2_d[e].rearrange("(c p) d -> p c d", p=P)).then_inc(we_in, 16)
            sp.dma_start(ow[:, :], ow_d.unsqueeze(0).to_broadcast([P, D])).then_inc(we_in, 16)
            sp.dma_start(ob[:, :], ob_d.unsqueeze(0).to_broadcast([P, D])).then_inc(we_in, 16)

            sp.wait_ge(scattered, 16 * K * T)
            def load_rows(i, u):
                sp.wait_ge(pe_xeT, i + 1)
                sp.dma_start(xg[:, u, :], xs_d[bass.ds(i * P, P), :]).then_inc(row_in[u], 16)

            with sp.Fori(0, NT // 2) as j:
                for u in range(2):
                    load_rows(j * 2 + u, u)
            load_rows(NT - 1, 0)
            with sp.Fori(0, NB) as b:
                sp.wait_ge(out_ready, b + 1)
                sp.wait_ge(stored, 16 * b + 32)
                sp.dma_start(out_d[bass.ds(b, 1)].rearrange("b (t p) d -> p (b t) d", p=P),
                             tok3(outb[:, bass.ds(b % 2, 1), :].rearrange("p a n -> p (a n)"))).then_inc(stored, 16)
            sp.wait_ge(stored, 16 * NB + 32)

        @block.gpsimd
        def _(pool):
            pool.memset(zeros[:, :], 0.0).then_inc(zero_set, 1)
            pool.memset(half[:, :], -0.5).then_inc(pool_const, 1)
            pool.memset(ones[:, :], 1.0).then_inc(pool_const, 1)
            pool.memset(kx[:, :, :, 0:W], 0.0).then_inc(pool_const, 1)
            pool.wait_ge(pool_const, 3)
            for n in range(2):
                pool.wait_ge(ln_in, n + 1)
                pool.tensor_tensor(lnt[:, 5 + n, :], lnt[:, 3 + n, :], half[:, :], ALU.pow).then_inc(ln_out, 1)
            pool.wait_ge(slots_ready, 1)
            pool.wait_ge(xs_zero, 16)
            pool.wait_ge(xh_ready, NB)
            for k in range(K):
                for t in range(T):
                    pool.indirect_dma_start(xs_d, bass.IndirectOffsetOnAxis(ap=sloti[:, k, t:t + 1], axis=0),
                                            xhat[:, t, :], None).then_inc(scattered, 16)
            pool.wait_ge(dve_xT, NB)
            with pool.Fori(0, NB) as b:
                pool.wait_ge(pe_gate, b + 1)
                pool.tensor_copy(xa[:, :], xn1T[:, bass.ds(b * SEQ, SEQ)]).then_inc(pool_xa, 1)
                pool.wait_ge(var_ready, b + 1)
                pool.tensor_tensor(ln2[:, 4, :], ln2[:, 3, :], half[:, 0:TB], ALU.pow).then_inc(rstd_ready, 1)
            for u in range(2):
                pool.wait_ge(row_out[u], 16 * ((NT + 1 - u) // 2) + 16)
            for b in range(NB + 1):
                if b < NB:
                    for t in range(TB * b, TB * b + TB):
                        for k in range(K):
                            pool.indirect_dma_start(rowsk[:, k, t, :], None, es_d,
                                                    bass.IndirectOffsetOnAxis(ap=sloti[:, k, t:t + 1], axis=0)
                                                    ).then_inc(gathered[b % 2], 16)
                if b:
                    pool.wait_ge(gathered[(b - 1) % 2], 16 * K * TB * ((b - 1) // 2 + 1))
                    pool.sem_inc(rows_ready, 1)
            with pool.Fori(0, NB) as b:
                pool.wait_ge(var3_ready, b + 1)
                pool.tensor_tensor(ln3[:, 4, :], ln3[:, 3, :], half[:, 0:TB], ALU.pow).then_inc(rstd3_ready, 1)

        @block.scalar
        def _(act):
            act.wait_ge(zero_set, 1)
            act.dma_start(xs_d.rearrange("(n p) d -> p n d", p=P),
                          zeros[:, :].unsqueeze(1).to_broadcast([P, NT, D])).then_inc(xs_zero, 16)
            act.wait_ge(w_in, 64)
            for b in range(NB):
                act.wait_ge(dve_xT, b + 1)
                if b >= 2:
                    act.wait_ge(pe_logit, b - 1)
                act.activation(xrT[:, b % 2, :], [GA, GB][b % 2][:, :], ACT.Identity, scale=vec[:, V_RW:V_RW + 1],
                               bias=vec[:, V_RB:V_RB + 1]).then_inc(act_xT, 1)
            act.wait_ge(diff_ready, 1)
            act.activation(gw[:, 2, :], gw[:, 3, :], ACT.Exp).then_inc(diff_exp, 1)

            act.sem_inc(act_gelu, FC)
            act.sem_inc(act_y, 1)
            act.wait_ge(pool_const, 3)
            with act.Fori(0, NB) as b:
                act.wait_ge(pe_q, b + 1)
                act.activation(qT[:, :], GA[:, :], ACT.Identity, scale=float(DH) ** -0.5).then_inc(act_q, 1)
                act.wait_ge(pe_k, b + 1)
                act.wait_ge(dve_kx, b + 1)
                act.activation(kT[:, :], GB[:, :], ACT.Identity).then_inc(act_k, 1)
                act.wait_ge(pe_drive, b + 1)
                act.wait_ge(dve_scan, b + 1)
                act.activation(drive[:, :], GC[:, :], ACT.Identity, bias=vec[:, V_BU:V_BU + 1]).then_inc(act_drive, 1)
                act.wait_ge(act_k, b + 1)
                act.wait_ge(pe_scores, NCH * b + NCH)
                for m in range(2, 4):
                    for g in range(HG):
                        act.activation(kx[:, m, g, W:], kT[:, :], ACT.Identity,
                                       scale=const[:, C_HEAD + 4 * g + m:C_HEAD + 4 * g + m + 1]).then_inc(act_kx, 1)
                act.wait_ge(pe_gate, b + 2)
                act.activation(gate[:, :], GB[:, :], ACT.Tanh, scale=0.5).then_inc(act_gate, 1)
                for c in range(NCH):
                    act.wait_ge(dve_sub, NCH * b + c + 3)
                    act.wait_ge(dve_pT, NCH * b + c + 1)
                    act.activation(pr[:, c % 2, :], sc[:, c % 2, :], ACT.Exp).then_inc(act_exp, 1)
                act.wait_ge(pe_y, b + 1)
                act.activation(yS[:, :], GA[:, :], ACT.Identity).then_inc(act_y, 1)
                act.wait_ge(pe_hT, b + 1)
                act.activation(hT[:, :], GB[:, :], ACT.Identity, scale=vec[:, V_G2:V_G2 + 1],
                               bias=vec[:, V_B2:V_B2 + 1]).then_inc(act_hT, 1)
                act.wait_ge(pe_mlp2, b + 1)
                for c in range(FC):
                    act.wait_ge(pe_mlp1, FC * b + c + 1)
                    act.activation(gT[:, c, :], [GC, GA, GB, GC][c][:, :], ACT.Gelu,
                                   bias=vec[:, V_M1 + c:V_M1 + c + 1]).then_inc(act_gelu, 1)

            def gelu(i, u):
                act.wait_ge(pe_he, i + 3)
                act.wait_ge(pe_heT, i + 1)
                act.activation(he[:, u, :], S[u][:, :], ACT.Gelu).then_inc(act_he, 1)

            def store(i, u):
                act.wait_ge(dve_eo, i + 3)
                act.dma_start(es_d[bass.ds(i * P, P), :], eo[:, u, :]).then_inc(row_out[u], 16)

            act.sem_inc(act_he, 2)
            gelu(0, 0)
            gelu(1, 1)
            with act.Fori(0, (NT - 3) // 2) as j:
                for u in range(2):
                    gelu(j * 2 + u + 2, u)
                    store(j * 2 + u, u)
            gelu(NT - 1, 0)
            for i in range(NT - 3, NT):
                store(i, i % 2)

        @block.tensor
        def _(pe):
            pe.wait_ge(w_in, 64)
            for b in range(NB):
                pe.wait_ge(xh_ready, b + 1)
                G = [GA, GB][b % 2]
                if b >= 2:
                    pe.wait_ge(act_xT, b - 1)
                    pe.wait_ge(dve_xT, b - 1)
                for t in range(TB):
                    last = nc.tensor.transpose(G[:, t * P:(t + 1) * P], xhat[:, b * TB + t, :], ident)
                last.then_inc(pe_xT, 1)
                pe.wait_ge(act_xT, b + 1)
                for t in range(TB):
                    n = b * TB + t
                    last = mm(GC[:, n * E:(n + 1) * E], xrT[:, b % 2, t * P:(t + 1) * P], rw[:, :],
                              start=True, stop=True)
                last.then_inc(pe_logit, 1)
            pe.wait_ge(picks_ready, 1)
            pe.wait_ge(pool_const, 3)
            mm(GA[:, 0:E * T], const[:, C_TRI:C_TRI + P], picks[:, :], start=True, stop=True)
            mm(GB[:, 0:E * T], ones[:, :], picks[:, :], start=True, stop=True).then_inc(pe_rank, 1)

            pe.sem_inc(pe_scores, NCH)
            pe.sem_inc(pe_gate, 1)
            pe.sem_inc(pe_pv, 1)
            pe.sem_inc(pe_mlp2, 1)
            pe.wait_ge(wm_in, 16 * 8)
            pe.wait_ge(dve_setup, 6)
            pe.wait_ge(slots_ready, 1)

            def bias_row(out, at):
                mm(out, sel0[:, :], rowp[:, at:at + D].unsqueeze(1).to_broadcast([RP, TB, D]),
                   start=True, stop=False, skip_group_check=True)

            def per_tile(out, lhs, rhs):
                for t in range(TB):
                    last = mm(out[:, t * P:(t + 1) * P], lhs[:, t * P:(t + 1) * P], rhs, start=False,
                              stop=(t == TB - 1), skip_group_check=True)
                return last

            with pe.Fori(0, NB) as b:
                pe.wait_ge(pool_xa, b + 1)
                pe.wait_ge(act_gelu, FC * b + 2)
                mm(GA[:, :], wqkv[:, 0:D], xa[:, :], start=True, stop=True).then_inc(pe_q, 1)
                pe.wait_ge(act_gelu, FC * b + 3)
                mm(GB[:, :], wqkv[:, D:2 * D], xa[:, :], start=True, stop=True).then_inc(pe_k, 1)
                pe.wait_ge(act_gelu, FC * b + 4)
                mm(GC[:, :], wdrive[:, :], xa[:, :], start=True, stop=True).then_inc(pe_drive, 1)
                pe.wait_ge(act_q, b + 1)
                wv = wqkv[:, 2 * D:3 * D].rearrange("p (g m d) -> p g m d", g=HG, m=4)
                for kb in range(NBLK):
                    for m in range(4):
                        last = mm(GA[m * W:(m + 1) * W, kb * W:(kb + 1) * W], xa[:, kb * W:(kb + 1) * W],
                                  wv[:, :, m, :], start=True, stop=True)
                last.then_inc(pe_v, 1)
                pe.wait_ge(act_k, b + 1)
                bias_row(GB[:, :], R_G)
                per_tile(GB, xa, wug[:, D:2 * D]).then_inc(pe_gate, 1)

                pe.wait_ge(dve_kx, b + 2)
                pe.wait_ge(act_kx, 8 * b + 8)

                def pv(kb, first):
                    n = 2 if kb + 1 < NBLK else 1
                    lo = pT[:, kb, 0, 1, :]
                    for g in range(HG):
                        rhs = bass.AP(lo.tensor, lo.offset + g * 2 * W, [list(lo.ap[0]), [HG * 2 * W - W, n], [1, W]])
                        last = mm(OV[g * W:(g + 1) * W, kb * W:(kb + n) * W], vx[:, kb, g * W:(g + 1) * W], rhs,
                                  start=first, stop=(kb == NBLK - 1), skip_group_check=True)
                    return last

                for c in range(NCH + 3):
                    if c < NCH:
                        pe.wait_ge(dve_sub, NCH * b + c + 1)
                        m0 = maskb[:, 0:4 * W].rearrange("p (a k) -> p a k", a=2).unsqueeze(2).to_broadcast([P, 2, HG, 2 * W]) \
                            if c == 0 else maskb[:, 2 * W:4 * W].unsqueeze(1).to_broadcast([P, 2 * HG, 2 * W])
                        mm(S[c % 2][:, :], identb[:, :], m0, start=True, stop=False, skip_group_check=True)
                        for k in range(2):
                            j = 2 * c + k
                            for m in range(4):
                                last = mm(S[c % 2][m * W:(m + 1) * W, k * 256:(k + 1) * 256],
                                          qT[:, j * W:(j + 1) * W], kx[:, m, :, j * W:(j + 2) * W],
                                          start=False, stop=(k == 1), skip_group_check=True)
                        last.then_inc(pe_scores, 1)
                    if c == 3:
                        pe.wait_ge(dve_scan, b + 2)
                        pe.wait_ge(dve_vx, b + 1)
                        pe.wait_ge(act_y, b + 1)
                        for t in range(TB):
                            last = mm(GA[:, t * P:(t + 1) * P], states[:, t * P:(t + 1) * P], cw[:, :],
                                      start=True, stop=True)
                        last.then_inc(pe_y, 1)
                        pe.wait_ge(dve_oT, b + 1)
                    if c >= 3:
                        n = c - 3
                        pe.wait_ge(dve_pT, NCH * b + n + 3)
                        if n:
                            pv(2 * n - 1, False)
                        last = pv(2 * n, n == 0)
                last = pv(NBLK - 1, False)
                last.then_inc(pe_pv, 1)
                for g in range(HG):
                    for s in range(2):
                        last = mm(DEN[g * W:(g + 1) * W, :], const[:, C_BLK:C_BLK + W], pT[:, :, g, s, :],
                                  start=(s == 0), stop=(s == 1), skip_group_check=True)
                last.then_inc(pe_den, 1)
                pe.wait_ge(dve_oT, b + 2)
                pe.wait_ge(act_drive, b + 1)
                bias_row(GC[:, :], R_O)
                per_tile(GC, oT, wo[:, :]).then_inc(pe_attn, 1)
                pe.wait_ge(act_gate, b + 1)
                pe.wait_ge(dve_h, b + 1)
                for t in range(TB):
                    last = nc.tensor.transpose(GB[:, t * P:(t + 1) * P], hh[:, t * P:(t + 1) * P], ident)
                last.then_inc(pe_hT, 1)
                pe.wait_ge(act_hT, b + 1)
                for c in range(FC):
                    if c == 0:
                        pe.wait_ge(dve_attn, b + 1)
                    if c == 1:
                        pe.wait_ge(act_y, b + 2)
                    if c == 3:
                        pe.wait_ge(act_gelu, FC * b + 5)
                    mm([GC, GA, GB, GC][c][:, :], m1[:, c * P:(c + 1) * P], hT[:, :], start=True, stop=True
                       ).then_inc(pe_mlp1, 1)
                pe.wait_ge(dve_acc, b + 1)
                bias_row(M2[:, :], R_M2)
                for c in range(FC):
                    pe.wait_ge(act_gelu, FC * b + c + 5)
                    for t in range(TB):
                        last = mm(M2[:, t * P:(t + 1) * P], gT[:, c, t * P:(t + 1) * P], m2[:, c, :],
                                  start=False, stop=(c == FC - 1), skip_group_check=True)
                last.then_inc(pe_mlp2, 1)

            pe.wait_ge(we_in, 16 * (2 * E + 2))
            pe.wait_ge(act_gelu, FC * NB + FC)
            pe.wait_ge(dve_acc, NB + 1)
            pe.sem_inc(pe_xeT, 2)
            pe.sem_inc(pe_heT, 2)
            pe.sem_inc(pe_eo, 2)
            pe.sem_inc(pe_he, 2)
            XT, HT, EO = [GA, GB], [OV, DEN], [GC, M2]

            def expert_of(i):
                return pe.value_load(texp[0:1, bass.ds(i, 1)], min_val=0, max_val=E - 1)

            def rows_T(i, u, h):
                pe.wait_ge(row_in[u], 16 * h + 16)
                pe.wait_ge(dve_xeT, i + 1)
                nc.tensor.transpose(XT[u][:, 0:P], xg[:, u, :], ident).then_inc(pe_xeT, 1)

            def layer1(i, u):
                e = expert_of(i)
                pe.wait_ge(dve_xeT, i + 3)
                pe.wait_ge(act_he, i + 1)
                mm(S[u][:, :], sel[:, 0, u, :], rowp[:, R_E1:R_E1 + FF], start=True, stop=False)
                mm(S[u][:, :], xeT[:, u, :], w1[:, bass.ds(e, 1), :].rearrange("p a f -> p (a f)"), start=False, stop=True).then_inc(pe_he, 1)

            def hidden_T(i, u):
                pe.wait_ge(act_he, i + 3)
                pe.wait_ge(dve_heT, i + 1)
                for c in range(FC):
                    last = nc.tensor.transpose(HT[u][:, c * P:(c + 1) * P], he[:, u, c * P:(c + 1) * P], ident)
                last.then_inc(pe_heT, 1)

            def layer2(i, u):
                e = expert_of(i)
                pe.wait_ge(dve_heT, i + 3)
                pe.wait_ge(dve_eo, i + 1)
                mm(EO[u][:, 0:D], sel[:, 1, u, :], rowp[:, R_E2:R_E2 + D], start=True, stop=False)
                for c in range(FC):
                    last = mm(EO[u][:, 0:D], heT[:, u, c * P:(c + 1) * P],
                              w2[:, bass.ds(e, 1), c, :].rearrange("p a f -> p (a f)"), start=False, stop=(c == FC - 1))
                last.then_inc(pe_eo, 1)

            rows_T(0, 0, 0)
            rows_T(1, 1, 0)
            layer1(0, 0)
            rows_T(2, 0, 1)
            layer1(1, 1)
            hidden_T(0, 0)
            with pe.Fori(0, (NT - 3) // 2) as j:
                for u in range(2):
                    i = j * 2 + u
                    rows_T(i + 3, 1 - u, j + 1 + u)
                    layer1(i + 2, u)
                    hidden_T(i + 1, 1 - u)
                    layer2(i, u)
            layer1(NT - 1, 0)
            hidden_T(NT - 2, 1)
            layer2(NT - 3, 0)
            hidden_T(NT - 1, 0)
            layer2(NT - 2, 1)
            layer2(NT - 1, 0)

        @block.vector
        def _(v):
            count = [0]
            link = chain(v, count)
            tt, ts, stt = v.tensor_tensor, v.tensor_scalar, v.scalar_tensor_tensor

            def moments(stats, out):
                me, ve, mo, vo = (stats[:, :, n] for n in (1, 2, 4, 5))
                tt(out[:, 0, :], me, mo, ALU.add).then_inc(dve, 1)
                tt(out[:, 1, :], me, mo, ALU.subtract).then_inc(dve, 1)
                tt(out[:, 2, :], ve, vo, ALU.add).then_inc(dve, 1)
                return 3

            v.wait_ge(x_in, 16)
            for t in range(T):
                ins = v.bn_stats(st[:, t, :], x[:, t, :])
            link(ins)
            count[0] += moments(st, lnt)
            v.wait_ge(dve, count[0])
            ts(lnt[:, 0, :], lnt[:, 0, :], 0.5, None, ALU.mult).then_inc(dve, 1)
            count[0] += 1
            link(tt(lnt[:, 1, :], lnt[:, 1, :], lnt[:, 1, :], ALU.mult))
            link(stt(lnt[:, 2, :], lnt[:, 1, :], D / 4, lnt[:, 2, :], ALU.mult, ALU.add))
            link(ts(lnt[:, 2, :], lnt[:, 2, :], 1.0 / D, None, ALU.mult))
            ts(lnt[:, 3, :], lnt[:, 2, :], EPS, None, ALU.add).then_inc(ln_in, 1)
            v.wait_ge(ln_out, 1)
            link(tt(lnt[:, 1, :], lnt[:, 5, :], lnt[:, 5, :], ALU.mult))
            link(tt(lnt[:, 2, :], lnt[:, 2, :], lnt[:, 1, :], ALU.mult))
            ts(lnt[:, 4, :], lnt[:, 2, :], EPS, None, ALU.add).then_inc(ln_in, 1)
            v.wait_ge(ln_out, 2)
            link(tt(lnt[:, 7, :], lnt[:, 5, :], lnt[:, 6, :], ALU.mult))

            v.wait_ge(w_in, 64)

            def feature_major(b):
                v.wait_ge(pe_xT, b + 1)
                ts(xn1T[:, b * SEQ:(b + 1) * SEQ], [GA, GB][b % 2][:, :], vec[:, V_G1:V_G1 + 1],
                   vec[:, V_B1:V_B1 + 1], ALU.mult, ALU.add).then_inc(dve_xT, 1)

            for b in range(NB):
                for t in range(TB * b, TB * b + TB):
                    ins = ts(xhat[:, t, :], x[:, t, :], lnt[:, 0, t:t + 1], lnt[:, 7, t:t + 1], ALU.subtract, ALU.mult)
                ins.then_inc(xh_ready, 1)
                for t in range(TB * b, TB * b + TB):
                    ins = ts(xn[:, t, :], x[:, t, :], lnt[:, 0, t:t + 1], lnt[:, 5, t:t + 1], ALU.subtract, ALU.mult)
                if b == NB - 1:
                    link(ins)
                if b:
                    feature_major(b - 1)
            feature_major(NB - 1)

            v.wait_ge(pe_logit, NB)
            link(tt(logit[:, :, :], GC[:, 0:T * E].rearrange("p (t e) -> p t e", e=E),
                    rb[:, :].unsqueeze(1).to_broadcast([P, T, E]), ALU.add))
            for t in range(T):
                ins = v.max(top[:, t, :], logit[:, t, :])
            link(ins)
            for t in range(T):
                ins = v.max_index(topi[:, t, :], top[:, t, :], logit[:, t, :])
            tt(gw[:, 3, :], top[:, :, 1], top[:, :, 0], ALU.subtract).then_inc(diff_ready, 1)
            link(ins)
            link(v.tensor_copy(topf[:, :, :].rearrange("p k t -> p t k"), topi[:, :, 0:K]))
            for k in range(K):
                ins = tt(pick[:, k, :, :], topf[:, k, :].unsqueeze(1).to_broadcast([P, E, T]),
                         const[:, C_IE:C_IE + E].unsqueeze(2).to_broadcast([P, E, T]), ALU.is_equal)
            link(ins)
            tt(picks[:, :].rearrange("p (e t) -> p e t", e=E), pick[:, 0, :, :], pick[:, 1, :, :], ALU.add
               ).then_inc(picks_ready, 1)
            v.wait_ge(diff_exp, 1)
            link(ts(gw[:, 3, :], gw[:, 2, :], 1.0, None, ALU.add))
            link(v.reciprocal(gw[:, 0, :], gw[:, 3, :]))
            link(tt(gw[:, 1, :], gw[:, 2, :], gw[:, 0, :], ALU.mult))
            v.wait_ge(pe_rank, 1)
            link(v.tensor_copy(tot[:, :], GB[:, 0:E * T]))
            link(v.tensor_tensor_scan(incl[:, :], const[:, C_RESET:C_RESET + E * T], tot[:, :], 0.0, ALU.mult, ALU.add))
            incl3 = incl[:, :].rearrange("p (e t) -> p e t", e=E)
            link(tt(cmpj[:, :, :], incl3[:, :, T - 1:T].to_broadcast([P, E, MB]),
                    const[:, C_J:C_J + MB].unsqueeze(1).to_broadcast([P, E, MB]), ALU.is_gt))
            link(v.tensor_reduce(blocks[:, 0, :], cmpj[:, :, :], AX_X, ALU.add))
            link(v.tensor_tensor_scan(blocks[:, 1, :], ones[:, 0:E], blocks[:, 0, :], 0.0, ALU.mult, ALU.add))
            link(tt(blocks[:, 2, :], blocks[:, 1, :], blocks[:, 0, :], ALU.subtract))
            link(ts(blocks[:, 3, :], blocks[:, 2, :], float(P), None, ALU.mult))
            link(tt(base[:, :], incl[:, :], tot[:, :], ALU.subtract))
            link(tt(base[:, :], base[:, :], GA[:, 0:E * T], ALU.add))
            link(tt(base[:, :].rearrange("p (e t) -> p e t", e=E), base[:, :].rearrange("p (e t) -> p e t", e=E),
                    blocks[:, 3, :].unsqueeze(2).to_broadcast([P, E, T]), ALU.add))
            for k in range(K):
                ins = tt(slotf[:, k, :, :], pick[:, k, :, :], base[:, :].rearrange("p (e t) -> p e t", e=E), ALU.mult)
            link(ins)
            for k in range(K):
                ins = v.tensor_reduce(slots[:, k, :], slotf[:, k, :, :].rearrange("p e t -> p t e"), AX_X, ALU.add)
            link(ins)
            v.tensor_copy(sloti[:, :, :], slots[:, :, :]).then_inc(dve, 1)
            count[0] += 1
            link(tt(tcmp[:, :, :], const[0:1, C_TI:C_TI + NT].unsqueeze(2).to_broadcast([1, NT, E]),
                    blocks[0:1, 1, :].unsqueeze(1).to_broadcast([1, NT, E]), ALU.is_ge))
            link(v.tensor_reduce(texpf[:, 0, :], tcmp[:, :, :], AX_X, ALU.add))
            link(ts(texpf[:, 1, :], texpf[:, 0, :], float(E - 1), None, ALU.min))
            v.tensor_copy(texp[:, :], texpf[:, 1, :]).then_inc(slots_ready, 1)

            v.wait_ge(wm_in, 16 * 8)
            tt(wdrive[:, :], bw[:, :], wug[:, 0:D], ALU.add).then_inc(dve_setup, 1)
            v.tensor_copy(identb[:, :], ident).then_inc(dve_setup, 1)
            v.tensor_copy(maskb[:, :], const[:, C_MASK:C_MASK + 4 * W]).then_inc(dve_setup, 1)
            link(v.tensor_copy(rowp[:, :], rowf[:, :]))
            link(tt(rowf[:, :], rowf[:, :], rowp[:, :], ALU.subtract))
            v.tensor_copy(rowp[QR:2 * QR, :], rowf[QR:2 * QR, :]).then_inc(dve_setup, 1)
            link(v.tensor_copy(rowp[2 * QR:RP, :], rowf[2 * QR:RP, :]))
            link(tt(rowf[2 * QR:RP, :], rowf[2 * QR:RP, :], rowp[2 * QR:RP, :], ALU.subtract))
            v.tensor_copy(rowp[2 * QR:RP, :], rowf[2 * QR:RP, :]).then_inc(dve_setup, 1)
            v.wait_ge(pool_const, 3)
            ts(sel0[:, :], ones[0:RP, :], const[0:RP, C_SEL:C_SEL + 1], None, ALU.mult).then_inc(dve_setup, 1)
            v.sem_inc(dve_sub, 2)
            v.sem_inc(dve_pT, 2)
            v.sem_inc(dve_oT, 1)
            v.sem_inc(dve_kx, 1)
            v.sem_inc(dve_scan, 1)
            v.sem_inc(dve_acc, 1)
            v.wait_ge(pool_const, 3)

            CH = 24
            with v.Fori(0, NB) as b:
                k0 = count[0]
                n = [0]

                def step(ins):
                    n[0] += 1
                    ins.then_inc(dve, 1)
                    v.wait_ge(dve, b * CH + k0 + n[0])

                v.wait_ge(act_k, b + 1)
                v.wait_ge(pe_scores, NCH * b + NCH)
                for m in range(2):
                    for g in range(HG):
                        ins = ts(kx[:, m, g, W:], kT[:, :], const[:, C_HEAD + 4 * g + m:C_HEAD + 4 * g + m + 1],
                                 None, ALU.mult)
                v.wait_ge(act_kx, 8 * b + 8)
                ins.then_inc(dve_kx, 1)
                v.wait_ge(pe_pv, b + 1)
                v.wait_ge(pe_v, b + 1)
                tt(vx[:, :, :].rearrange("p k (g m d) -> p (k g) m d", g=HG, m=4),
                   GA[:, :].rearrange("p (n d) -> p n d", d=DH).unsqueeze(2).to_broadcast([P, NBLK * HG, 4, DH]),
                   const[:, C_BLK:C_BLK + W].rearrange("p (m d) -> p m d", m=4).unsqueeze(1).to_broadcast(
                       [P, NBLK * HG, 4, DH]), ALU.mult).then_inc(dve_vx, 1)
                v.wait_ge(act_drive, b + 1)
                v.tensor_tensor_scan(states[:, :], vec[:, V_A:V_A + 1].to_broadcast([P, SEQ]), drive[:, :], 0.0,
                                     ALU.mult, ALU.add).then_inc(dve_scan, 1)
                for c in range(NCH + 1):
                    if c < NCH:
                        s3 = S[c % 2][:, :].rearrange("p (u k) -> p u k", u=8)
                        v.wait_ge(pe_scores, NCH * b + NCH + c + 1)
                        v.tensor_reduce(smax[:, c % 2, :], s3, AX_X, ALU.max).then_inc(dve_max, 1)
                        v.wait_ge(dve_max, NCH * b + c + 1)
                        if c >= 2:
                            v.wait_ge(act_exp, NCH * b + c - 1)
                        tt(sc[:, c % 2, :].rearrange("p (u k) -> p u k", u=8), s3,
                           smax[:, c % 2, :].unsqueeze(2).to_broadcast([P, 8, 2 * W]), ALU.subtract
                           ).then_inc(dve_sub, 1)
                    if c >= 1:
                        i = c - 1
                        v.wait_ge(act_exp, NCH * b + i + 1)
                        v.transpose(pT[:, 2 * i:2 * i + 2, :, :, :].rearrange("p a g s q -> p (a g s q)"),
                                    pr[:, i % 2, :]).then_inc(dve_pT, 1)
                v.wait_ge(pe_den, b + 1)
                v.reciprocal(rden[:, :], DEN[:, :]).then_inc(dve_rden, 1)
                v.wait_ge(dve_rden, b + 1)
                tt(oT[:, :], OV[:, :], rden[:, :], ALU.mult).then_inc(dve_oT, 1)
                v.wait_ge(act_y, b + 2)
                step(tt(mix[:, 0, :], yS[:, :], xn[:, bass.ds(b * TB, TB), :].rearrange("p t d -> p (t d)"), ALU.add))
                v.wait_ge(pe_attn, b + 1)
                tt(mix[:, 1, :], GC[:, :], yS[:, :], ALU.subtract).then_inc(dve_attn, 1)
                v.wait_ge(dve_attn, b + 1)
                v.wait_ge(act_gate, b + 1)
                step(stt(mix[:, 2, :], gate[:, :], 1.0, mix[:, 1, :], ALU.add, ALU.mult))
                step(stt(x2[:, :], mix[:, 2, :], 0.5, mix[:, 0, :], ALU.mult, ALU.add))
                for t in range(TB):
                    ins = v.bn_stats(st2[:, t, :], x2[:, t * D:(t + 1) * D])
                step(ins)
                n[0] += moments(st2, ln2)
                v.wait_ge(dve, b * CH + k0 + n[0])
                step(ts(ln2[:, 0, :], ln2[:, 0, :], 0.5, None, ALU.mult))
                step(tt(ln2[:, 1, :], ln2[:, 1, :], ln2[:, 1, :], ALU.mult))
                step(stt(ln2[:, 2, :], ln2[:, 1, :], D / 4, ln2[:, 2, :], ALU.mult, ALU.add))
                ts(ln2[:, 3, :], ln2[:, 2, :], 1.0 / D, EPS, ALU.mult, ALU.add).then_inc(var_ready, 1)
                v.wait_ge(rstd_ready, b + 1)
                for t in range(TB):
                    ins = ts(hh[:, t * D:(t + 1) * D], x2[:, t * D:(t + 1) * D], ln2[:, 0, t:t + 1],
                             ln2[:, 4, t:t + 1], ALU.subtract, ALU.mult)
                ins.then_inc(dve_h, 1)
                step(tt(mix[:, 0, :], x2[:, :], x[:, bass.ds(b * TB, TB), :].rearrange("p t d -> p (t d)"), ALU.add))
                v.wait_ge(pe_mlp2, b + 2)
                v.wait_ge(scattered, 16 * K * T)
                tt(acc[:, bass.ds(b * TB, TB), :].rearrange("p t d -> p (t d)"), M2[:, :], mix[:, 0, :], ALU.add
                   ).then_inc(dve_acc, 1)
                for _ in range(CH - n[0]):
                    v.sem_inc(dve, 1)
            count[0] += CH * NB

            v.wait_ge(slots_ready, 1)
            v.wait_ge(we_in, 16 * (2 * E + 2))
            v.sem_inc(dve_xeT, 2)
            v.sem_inc(dve_heT, 2)
            v.sem_inc(dve_eo, 2)
            XT, HT, EO = [GA, GB], [OV, DEN], [GC, M2]

            def rows_T(i, u):
                e = v.value_load(texp[0:1, bass.ds(i, 1)], min_val=0, max_val=E - 1)
                v.wait_ge(pe_xeT, i + 3)
                v.wait_ge(pe_he, i + 1)
                ts(sel[:, 0, u, :], ones[0:RP, :], const[0:RP, bass.ds(e + C_SEL, 1)], None, ALU.mult)
                ts(xeT[:, u, :], XT[u][:, 0:P], vec[:, bass.ds(e + V_EW, 1)], vec[:, bass.ds(e + V_EB, 1)],
                   ALU.mult, ALU.add).then_inc(dve_xeT, 1)

            def hidden_T(i, u):
                e = v.value_load(texp[0:1, bass.ds(i, 1)], min_val=0, max_val=E - 1)
                v.wait_ge(pe_heT, i + 3)
                v.wait_ge(pe_eo, i + 1)
                ts(sel[:, 1, u, :], ones[0:RP, :], const[0:RP, bass.ds(e + C_SEL, 1)], None, ALU.mult)
                v.tensor_copy(heT[:, u, :], HT[u][:, :]).then_inc(dve_heT, 1)

            def finish(i, u, h):
                v.wait_ge(pe_eo, i + 3)
                v.wait_ge(row_out[u], 16 * h + 16)
                v.tensor_copy(eo[:, u, :], EO[u][:, 0:D]).then_inc(dve_eo, 1)

            v.sem_inc(row_out[0], 16)
            v.sem_inc(row_out[1], 16)
            rows_T(0, 0)
            rows_T(1, 1)
            rows_T(2, 0)
            hidden_T(0, 0)
            with v.Fori(0, (NT - 3) // 2) as j:
                for u in range(2):
                    i = j * 2 + u
                    rows_T(i + 3, 1 - u)
                    hidden_T(i + 1, 1 - u)
                    finish(i, u, j)
            hidden_T(NT - 2, 1)
            finish(NT - 3, 0, NT // 2 - 1)
            hidden_T(NT - 1, 0)
            finish(NT - 2, 1, NT // 2 - 1)
            finish(NT - 1, 0, NT // 2)

            v.sem_inc(stored, 32)
            C3 = 20
            k1 = count[0]
            with v.Fori(0, NB) as b:
                n = [0]

                def step(ins):
                    n[0] += 1
                    ins.then_inc(dve, 1)
                    v.wait_ge(dve, b * C3 + k1 + n[0])

                v.wait_ge(rows_ready, b + 1)
                for k in range(K):
                    ins = tt(tok3(comb[:, k, :]), rowsk[:, k, bass.ds(b * TB, TB), :],
                             gw[:, k, bass.ds(b * TB, TB)].unsqueeze(2).to_broadcast([P, TB, D]), ALU.mult)
                step(ins)
                step(tt(comb[:, 2, :], comb[:, 0, :], comb[:, 1, :], ALU.add))
                for t in range(TB):
                    ins = v.bn_stats(st3[:, t, :], comb[:, 2, t * D:(t + 1) * D])
                step(ins)
                n[0] += moments(st3, ln3)
                v.wait_ge(dve, b * C3 + k1 + n[0])
                step(ts(ln3[:, 0, :], ln3[:, 0, :], 0.5, None, ALU.mult))
                step(tt(ln3[:, 1, :], ln3[:, 1, :], ln3[:, 1, :], ALU.mult))
                step(stt(ln3[:, 2, :], ln3[:, 1, :], D / 4, ln3[:, 2, :], ALU.mult, ALU.add))
                ts(ln3[:, 3, :], ln3[:, 2, :], 1.0 / D, EPS, ALU.mult, ALU.add).then_inc(var3_ready, 1)
                v.wait_ge(rstd3_ready, b + 1)
                for t in range(TB):
                    ins = ts(comb[:, 0, t * D:(t + 1) * D], comb[:, 2, t * D:(t + 1) * D], ln3[:, 0, t:t + 1],
                             ln3[:, 4, t:t + 1], ALU.subtract, ALU.mult)
                step(ins)
                step(tt(tok3(comb[:, 1, :]), tok3(comb[:, 0, :]), ow[:, :].unsqueeze(1).to_broadcast([P, TB, D]), ALU.mult))
                step(tt(tok3(comb[:, 0, :]), tok3(comb[:, 1, :]), ob[:, :].unsqueeze(1).to_broadcast([P, TB, D]), ALU.add))
                v.wait_ge(stored, 16 * b + 16)
                tt(outb[:, bass.ds(b % 2, 1), :].rearrange("p a n -> p (a n)"),
                   comb[:, 0, :], acc[:, bass.ds(b * TB, TB), :].rearrange("p t d -> p (t d)"), ALU.add
                   ).then_inc(out_ready, 1)
                v.wait_ge(out_ready, b + 1)
                for _ in range(C3 - n[0]):
                    v.sem_inc(dve, 1)


def kernel(**inputs):
    import concourse.bacc as _bacc
    from concourse.bass_utils import run_bass_kernel_spmd as _run

    a = {k: np.ascontiguousarray(v) for k, v in inputs.items()}

    def at(n):
        return a["L0_attn_" + n]

    def ft(n):
        return a["L0_ffn_" + n]

    bug = at("b_ug")
    vec = np.concatenate(
        [np.stack([at("ln1_g"), at("ln1_b"), at("ln2_g"), at("ln2_b"), bug[:D], at("A"), ft("router_ln_w"),
                   ft("router_ln_b")]), at("mlp_b1").reshape(FC, P), ft("exp_ln_w"), ft("exp_ln_b")]).T
    row = np.zeros((3, QR, R_N), np.float32)
    for at_, n in ((R_G, bug[D:]), (R_O, at("b_O")), (R_M2, at("mlp_b2"))):
        row[:, 0, at_:at_ + D] = n
    row[:, :E, R_E1:R_E1 + FF] = ft("b1")
    row[:, :E, R_E2:R_E2 + D] = ft("b2")
    arrays = {
        "x": at("x"), "const": constants(), "vec": np.ascontiguousarray(vec), "row": row.reshape(RP, R_N),
        "wqkv": at("W_qkv"), "wo": at("W_O"), "wug": at("W_ug"), "bw": at("B_w"), "cw": at("C_w"),
        "m1": at("mlp_W1"), "m2": at("mlp_W2"), "rw": ft("router_w"), "rb": ft("router_b"), "w1": ft("w1"),
        "w2": ft("w2"), "ow": ft("out_ln_w"), "ob": ft("out_ln_b"),
    }
    nc = _bacc.Bacc("TRN2", target_bir_lowering=False, num_devices=1)
    args = [nc.dram_tensor(f"in_{n}", v.shape, mybir.dt.from_np(v.dtype), kind="ExternalInput").ap()
            for n, v in arrays.items()]
    out = nc.dram_tensor("out_0", (NB, SEQ, D), F32, kind="ExternalOutput").ap()
    program(nc, *args, out)
    r = _run(nc, [{f"in_{n}": v for n, v in arrays.items()}], core_ids=[0])
    return r.results[0]["out_0"]
```

```python
from contextlib import ExitStack

import numpy as np

import concourse.bass as bass
from concourse import mybir

ALU = mybir.AluOpType
ACT = mybir.ActivationFunctionType
F32 = mybir.dt.float32
BF16 = mybir.dt.bfloat16
I32 = mybir.dt.int32
U32 = mybir.dt.uint32
AX_X = mybir.AxisListType.X

P = 128
D = 128
NB, SEQ = 4, 512
T = NB * SEQ // P
TB = SEQ // P
H, DH = 16, 8
HG = 4
W = 32
NBLK = SEQ // W
NCH = NBLK // 2
E, FF, K = 8, 512, 2
FC = FF // P
NT = (NB * SEQ * K) // P + E - 1
MB = NB * SEQ // P
EPS = 1e-5
NEG = -1e30

C_ID = 0
C_TRI = C_ID + P
C_HEAD = C_TRI + P
C_BLK = C_HEAD + H
C_MASK = C_BLK + W
C_RESET = C_MASK + 4 * W
C_IE = C_RESET + E * T
C_J = C_IE + E
C_TI = C_J + MB
C_SEL = C_TI + NT
C_ONE = C_SEL + 1
C_N = C_ONE + E
V_G1, V_B1, V_G2, V_B2, V_BU, V_A, V_RW, V_RB = range(8)
V_M1 = 8
V_N = V_M1 + FC
K_W1 = 0
K_W2 = K_W1 + FF
K_EW = K_W2 + FC * D
K_EB = K_EW + 1
K_B1 = K_EB + 1
K_B2 = K_B1 + FC
K_N = K_B2 + D
R_G, R_O, R_M2, R_OB = 0, D, 2 * D, 3 * D
R_N = 4 * D
QR = 32
RP = 3 * QR
RING = 4
STEPS = 16
LEAD = 7
MAGIC = 0x5F3759DF


def constants():
    c = np.zeros((P, C_N), np.float32)
    p = np.arange(P)
    c[:, C_ID:C_ID + P] = np.eye(P)
    c[:, C_TRI:C_TRI + P] = p[:, None] < p[None, :]
    c[:, C_HEAD:C_HEAD + H] = p[:, None] // DH == np.arange(H)[None, :]
    c[:, C_BLK:C_BLK + W] = p[:, None] // W == np.arange(W)[None, :] // DH
    q, k = p[:, None] % W, np.arange(2 * W)[None, :]
    band = (k > q) & (k <= q + W)
    c[:, C_MASK:C_MASK + 2 * W] = np.where(band & (k >= W), 0.0, NEG)
    c[:, C_MASK + 2 * W:C_MASK + 4 * W] = np.where(band, 0.0, NEG)
    c[:, C_RESET:C_RESET + E * T] = np.arange(E * T)[None, :] % T != 0
    c[:, C_IE:C_IE + E] = np.arange(E)
    c[:, C_J:C_J + MB] = np.arange(MB) * P
    c[:, C_TI:C_TI + NT] = np.arange(NT)
    c[:, C_ONE:C_ONE + E] = 1.0
    c[:, C_SEL] = p % QR == 0
    return c


def program(nc, x_d, const_d, vec_d, row_d, wqkv_d, wo_d, wug_d, bw_d, cw_d, m1_d, m2_d,
            rw_d, rb_d, pk_d, ow_d, out_d):
    xs_d = nc.dram_tensor("sorted_rows", (NT * P, D), F32).ap()
    es_d = nc.dram_tensor("expert_rows", (NT * P, D), F32).ap()
    mm = nc.tensor.matmul
    ctx = ExitStack()
    with ctx:
        def sb(name, shape, dt=F32):
            return ctx.enter_context(nc.sbuf_tensor(name, shape, dt))

        def bank(name):
            return ctx.enter_context(nc.psum_tensor(name, [P, 512], F32))

        def sem(name):
            return ctx.enter_context(nc.semaphore(name))

        const = sb("const", [P, C_N])
        vec = sb("vec", [P, V_N])
        rowp = sb("rowp", [RP, R_N], BF16)
        sel0 = sb("sel0", [RP, P], BF16)
        wqkv = sb("wqkv", [P, 3 * D])
        wo = sb("wo", [P, D])
        wug = sb("wug", [P, 2 * D])
        bw = sb("bw", [P, D])
        cw = sb("cw", [P, D])
        m1 = sb("m1", [P, FF])
        m2 = sb("m2", [P, FC, D])
        rw = sb("rw", [P, E])
        rb = sb("rb", [P, E])
        ow = sb("ow", [P, D])
        wdrive = sb("wdrive", [P, D])
        identb = sb("identb", [P, P], BF16)
        maskb = sb("maskb", [P, 4 * W], BF16)
        ones = sb("ones", [P, P])
        zeros = sb("zeros", [P, D])
        half = sb("half", [P, T // 2])
        ident = const[:, C_ID:C_ID + P]

        x = sb("x", [P, T, D])
        xn = sb("xn", [P, T, D])
        xhat = sb("xhat", [P, T, D])
        xn1T = sb("xn1T", [P, T * P])
        acc = xhat

        st = sb("st", [P, T, 6])
        lnt = sb("lnt", [P, 12, T])
        topf = sb("topf", [P, K, T])
        gw = sb("gw", [P, 4, T])
        blocks = sb("blocks", [P, 4, E])
        slots = sb("slots", [P, K, T])
        sloti = sb("sloti", [P, K, T], I32)
        tcmp = sb("tcmp", [1, NT, E])
        texpf = sb("texpf", [1, 2, NT])
        texp = sb("texp", [1, NT], I32)

        xa = sb("xa", [P, SEQ])
        qT = sb("qT", [P, SEQ])
        kT = sb("kT", [P, SEQ])
        kx = sb("kx", [P, 4, HG, W + SEQ])
        vx = sb("vx", [P, NBLK, D])
        drive = sb("drive", [P, SEQ])
        states = sb("states", [P, SEQ])
        gate = sb("gate", [P, SEQ])
        smax = sb("smax", [P, 2, 8])
        sc = sb("sc", [P, 2, 512])
        pr = sb("pr", [P, 2, 512])
        xrT = pr
        pT = sb("pT", [P, NBLK, HG, 2, W])
        rden = sb("rden", [P, SEQ])
        oT = sb("oT", [P, SEQ])
        yS = sb("yS", [P, SEQ])
        mix = sb("mix", [P, 3, SEQ])
        x2 = sb("x2", [P, SEQ])
        st2 = sb("st2", [P, TB, 6])
        ln2 = sb("ln2", [P, 8, TB])
        hh = sb("hh", [P, SEQ])
        hT = sb("hT", [P, SEQ])
        gT = sb("gT", [P, FC, SEQ])
        rowf = sc[0:RP, 0, 0:R_N]
        ET = E * T
        early = gT[:, :, :].rearrange("p c n -> p (c n)")
        logit = early[:, 0:ET].rearrange("p (t e) -> p t e", e=E)
        top = early[:, ET:2 * ET].rearrange("p (t e) -> p t e", e=8)
        topi = early[:, 2 * ET:3 * ET].bitcast(U32).rearrange("p (t e) -> p t e", e=8)
        pick = early[:, 3 * ET:5 * ET].rearrange("p (k e t) -> p k e t", k=K, e=E)
        picks, tot, incl, base = (early[:, n * ET:(n + 1) * ET] for n in range(5, 9))
        slotf = early[:, 9 * ET:11 * ET].rearrange("p (k e t) -> p k e t", k=K, e=E)
        cmpj = early[:, 11 * ET:11 * ET + E * MB].rearrange("p (e j) -> p e j", e=E)

        xg = sb("xg", [P, RING, D])
        pk = sb("pk", [P, RING * K_N])
        xeT = sb("xeT", [P, 2, P])
        heT = sb("heT", [P, 2, FF])
        eo = sb("eo", [P, RING, D])

        rowsk = pk[:, 0:K * T * D].rearrange("p (k t d) -> p k t d", k=K, t=T)
        comb = sb("comb", [P, T, D])
        st3 = sb("st3", [P, T // 2, 6])
        ln3 = sb("ln3", [P, 4, T // 2])
        rstd3 = sb("rstd3", [P, T])

        GA, GB, GC = bank("GA"), bank("GB"), bank("GC")
        S = [bank("S0"), bank("S1")]
        OV, XT, EO = bank("OV"), bank("XT"), bank("EO")
        XT4 = [GA, GB, S[0], S[1]]

        x_in = [sem(f"x_in{b}") for b in range(NB)]
        w_in = sem("w_in")
        wm_in = sem("wm_in")
        wo_in = sem("wo_in")
        xs_zero = sem("xs_zero")
        zero_set = sem("zero_set")
        scattered = sem("scattered")
        row_in = [sem(f"row_in{n}") for n in range(RING)]
        pk_in = [sem(f"pk_in{n}") for n in range(RING)]
        row_out = [sem(f"row_out{n}") for n in range(RING)]
        gathered = [sem(f"gathered{b}") for b in range(NB)]
        texp_ready = sem("texp_ready")
        stored = sem("stored")
        pool_const = sem("pool_const")
        xa_ready = sem("xa_ready")
        dve = sem("dve_chain")
        comb_chain = sem("comb_chain")
        dve_setup = sem("dve_setup")
        xh_ready = sem("xh_ready")
        pe_xT = sem("pe_xT")
        act_xT = sem("act_xT")
        act_xn = sem("act_xn")
        nmr_ready = sem("nmr_ready")
        norm1 = sem("norm1")
        act_weigh = sem("act_weigh")
        gates = sem("gates")
        logit_read = sem("logit_read")
        pe_logit = sem("pe_logit")
        diff_ready = sem("diff_ready")
        diff_exp = sem("diff_exp")
        picks_ready = sem("picks_ready")
        pe_rank = sem("pe_rank")
        slots_ready = sem("slots_ready")
        pe_q, pe_k, pe_drive, pe_v, pe_gate = sem("pe_q"), sem("pe_k"), sem("pe_drive"), sem("pe_v"), sem("pe_gate")
        pe_scores, pe_pv, pe_den, pe_y, pe_attn = sem("pe_scores"), sem("pe_pv"), sem("pe_den"), sem("pe_y"), sem("pe_attn")
        pe_hT, pe_mlp1, pe_mlp2 = sem("pe_hT"), sem("pe_mlp1"), sem("pe_mlp2")
        act_q, act_k, act_kx, act_drive, act_gate = sem("act_q"), sem("act_k"), sem("act_kx"), sem("act_drive"), sem("act_gate")
        act_exp, act_y, act_hT, act_gelu = sem("act_exp"), sem("act_y"), sem("act_hT"), sem("act_gelu")
        dve_kx, dve_vx, dve_scan, dve_max = sem("dve_kx"), sem("dve_vx"), sem("dve_scan"), sem("dve_max")
        dve_sub, dve_pT, dve_rden, dve_oT = sem("dve_sub"), sem("dve_pT"), sem("dve_rden"), sem("dve_oT")
        dve_attn, dve_h, dve_acc = sem("dve_attn"), sem("dve_h"), sem("dve_acc")
        var_ready, rstd_ready = sem("var_ready"), sem("rstd_ready")
        pe_xeT, dve_xeT, pe_he, act_he, pe_eo, dve_eo = (
            sem("pe_xeT"), sem("dve_xeT"), sem("pe_he"), sem("act_he"), sem("pe_eo"), sem("dve_eo"))
        var3_ready, rstd3_ready, out_ready = sem("var3_ready"), sem("rstd3_ready"), sem("out_ready")

        block = ctx.enter_context(nc.Block())

        def tok3(ap):
            return ap.rearrange("p (t d) -> p t d", d=D)

        def chain(eng, count):
            def link(ins):
                count[0] += 1
                ins.then_inc(dve, 1)
                eng.wait_ge(dve, count[0])
            return link

        def after(t, k):
            return t[0], t[1] + k

        def tile(t):
            return t[0] * RING + t[1]

        def turn_of(t):
            return t[0] + t[1] // RING

        def exists(t):
            return not isinstance(t[0], int) or 0 <= tile(t) < NT

        def need(eng, semaphore, value):
            if not isinstance(value, int) or value > 0:
                eng.wait_ge(semaphore, value)

        def spread(b):
            heads = [(m, g) for m in range(4) for g in range(HG)]
            n = 4 if isinstance(b, int) and b == 0 else 10
            return heads[:n], heads[n:]

        def sequences(eng, attend, step, start=lambda n: None, end=lambda n: None):
            first = LEAD - 2
            attend(0, lambda n: step((0, n - STEPS + first)) if n >= STEPS - LEAD else start(n))
            with eng.Fori(1, NB - 1) as b:
                attend(b, lambda n: step(((b - 1) * (STEPS // RING), first + n)))
            drain = NT - first - (NB - 2) * STEPS
            attend(NB - 1, lambda n: step((0, NT - drain + n)) if n < drain else end(n))

        @block.sync
        def _(sp):
            for b in range(NB):
                sp.dma_start(x[:, b * TB:(b + 1) * TB, :], x_d[b].rearrange("(t p) d -> p t d", p=P)
                             ).then_inc(x_in[b], 16)
            for dst, src in ((const[:, :], const_d), (vec[:, :], vec_d), (rw[:, :], rw_d),
                             (rb[:, :], rb_d.unsqueeze(0).to_broadcast([P, E]))):
                sp.dma_start(dst, src).then_inc(w_in, 16)
            for dst, src in ((wqkv[:, :], wqkv_d), (wug[:, :], wug_d), (bw[:, :], bw_d), (rowf, row_d)):
                sp.dma_start(dst, src).then_inc(wm_in, 16)
            for dst, src in ((wo[:, :], wo_d), (cw[:, :], cw_d), (m1[:, :], m1_d),
                             (m2[:, :, :], m2_d.rearrange("(c p) d -> p c d", p=P)),
                             (ow[:, :], ow_d.unsqueeze(0).to_broadcast([P, D]))):
                sp.dma_start(dst, src).then_inc(wo_in, 16)
            sp.wait_ge(zero_set, 1)
            sp.dma_start(xs_d.rearrange("(n p) d -> p n d", p=P),
                         zeros[:, :].unsqueeze(1).to_broadcast([P, NT, D])).then_inc(xs_zero, 16)

            def load_packet(t):
                u = t[1] % RING
                need(sp, dve_eo, tile(t) - RING + 1)
                e = sp.value_load(texp[0:1, bass.ds(tile(t), 1)], min_val=0, max_val=E - 1)
                sp.dma_start(pk[:, u * K_N:(u + 1) * K_N], pk_d[bass.ds(e, 1)].rearrange("a p n -> p (a n)")
                             ).then_inc(pk_in[u], 16)

            def load_rows(t):
                u = t[1] % RING
                need(sp, pe_xeT, tile(t) - RING + 1)
                sp.dma_start(xg[:, u, :], xs_d[bass.ds(tile(t) * P, P), :]).then_inc(row_in[u], 16)

            def store(t):
                sp.wait_ge(dve_eo, tile(t) + 1)
                sp.dma_start(es_d[bass.ds(tile(t) * P, P), :], eo[:, t[1] % RING, :]
                             ).then_inc(row_out[t[1] % RING], 16)

            sp.wait_ge(texp_ready, 1)
            for n in range(RING):
                load_packet((0, n))
            sp.wait_ge(scattered, 16 * K * T)
            for n in range(RING):
                load_rows((0, n))
            quads = (NT - RING) // RING
            with sp.Fori(0, quads) as j:
                for u in range(RING):
                    load_rows((j, u + RING))
                    load_packet((j, u + RING))
                    store((j, u))
            for n in range(quads * RING, NT):
                if n + RING < NT:
                    load_rows((0, n + RING))
                    load_packet((0, n + RING))
                store((0, n))
            for b in range(NB):
                sp.wait_ge(out_ready, b + 1)
                sp.dma_start(out_d[b].rearrange("(t p) d -> p t d", p=P), comb[:, b * TB:(b + 1) * TB, :]
                             ).then_inc(stored, 16)
            sp.wait_ge(stored, 16 * NB)

        @block.gpsimd
        def _(pool):
            pool.memset(zeros[:, :], 0.0).then_inc(zero_set, 1)
            pool.memset(half[:, :], -0.5).then_inc(pool_const, 1)
            pool.memset(ones[:, :], 1.0).then_inc(pool_const, 1)
            pool.memset(kx[:, :, :, 0:W], 0.0).then_inc(pool_const, 1)
            pool.wait_ge(pool_const, 3)
            pool.wait_ge(slots_ready, 1)
            pool.wait_ge(xs_zero, 16)
            pool.wait_ge(xh_ready, NB)
            for k in range(K):
                for t in range(T):
                    pool.indirect_dma_start(xs_d, bass.IndirectOffsetOnAxis(ap=sloti[:, k, t:t + 1], axis=0),
                                            xhat[:, t, :], None).then_inc(scattered, 16)

            def norm2(b):
                pool.wait_ge(var_ready, b + 1)
                pool.tensor_tensor(ln2[:, 4, :], ln2[:, 3, :], half[:, 0:TB], ALU.pow).then_inc(rstd_ready, 1)

            with pool.Fori(0, NB - 1) as b:
                norm2(b)
            for u in range(RING):
                pool.wait_ge(row_out[u], 16 * ((NT - 1 - u) // RING + 1))
            for b in range(NB):
                if b == NB - 1:
                    norm2(NB - 1)
                for t in range(TB * b, TB * b + TB):
                    for k in range(K):
                        pool.indirect_dma_start(rowsk[:, k, t, :], None, es_d,
                                                bass.IndirectOffsetOnAxis(ap=sloti[:, k, t:t + 1], axis=0)
                                                ).then_inc(gathered[b], 16)
            for h in range(2):
                pool.wait_ge(var3_ready, h + 1)
                pool.tensor_tensor(rstd3[:, h * T // 2:(h + 1) * T // 2], ln3[:, 3, :], half[:, :], ALU.pow
                                   ).then_inc(rstd3_ready, 1)

        @block.scalar
        def _(act):
            def norm(tiles):
                for t in tiles:
                    ins = act.activation(xn[:, t, :], x[:, t, :], ACT.Identity, scale=lnt[:, 5, t:t + 1],
                                         bias=lnt[:, 10, t:t + 1])
                ins.then_inc(norm1, 1)

            act.wait_ge(nmr_ready, 1)
            norm(range(T // 4))
            act.wait_ge(w_in, 64)
            for b in range(NB):
                act.wait_ge(pe_xT, b + 1)
                if b >= 2:
                    act.wait_ge(pe_logit, b - 1)
                act.activation(xrT[:, b % 2, :], XT4[b][:, :], ACT.Identity,
                               scale=vec[:, V_RW:V_RW + 1], bias=vec[:, V_RB:V_RB + 1]).then_inc(act_xT, 1)
                act.activation(xa[:, :] if b == 0 else xn1T[:, b * SEQ:(b + 1) * SEQ], XT4[b][:, :], ACT.Identity,
                               scale=vec[:, V_G1:V_G1 + 1], bias=vec[:, V_B1:V_B1 + 1]
                               ).then_inc(xa_ready if b == 0 else act_xn, 1)

            norm(range(T // 4, T))

            def start(n):
                if n == 1:
                    act.wait_ge(diff_ready, 1)
                    act.activation(gw[:, 2, :], gw[:, 3, :], ACT.Exp).then_inc(diff_exp, 1)

            act.sem_inc(act_gelu, FC)
            act.sem_inc(act_y, 1)
            act.wait_ge(pool_const, 3)

            def attend(b, beside):
                act.wait_ge(pe_q, b + 1)
                act.activation(qT[:, :], GA[:, :], ACT.Identity, scale=float(DH) ** -0.5).then_inc(act_q, 1)
                act.wait_ge(pe_k, b + 1)
                act.wait_ge(dve_kx, b + 1)
                need(act, act_kx, b)
                act.activation(kT[:, :], GB[:, :], ACT.Identity).then_inc(act_k, 1)
                beside(0)
                act.wait_ge(pe_drive, b + 1)
                act.wait_ge(dve_scan, b + 1)
                act.activation(drive[:, :], GC[:, :], ACT.Identity, bias=vec[:, V_BU:V_BU + 1]).then_inc(act_drive, 1)
                act.wait_ge(act_k, b + 1)
                act.wait_ge(pe_scores, NCH * b + NCH)
                mine = spread(b)[1]
                for i, (m, g) in enumerate(mine):
                    ins = act.activation(kx[:, m, g, W:], kT[:, :], ACT.Identity,
                                         scale=const[:, C_HEAD + 4 * g + m:C_HEAD + 4 * g + m + 1])
                    if i == len(mine) - 3:
                        beside(1)
                ins.then_inc(act_kx, 1)
                act.wait_ge(pe_gate, b + 2)
                act.activation(gate[:, :], GB[:, :], ACT.Tanh, scale=0.5).then_inc(act_gate, 1)
                beside(2)
                beside(3)
                for c in range(NCH):
                    act.wait_ge(dve_sub, NCH * b + c + 3)
                    act.wait_ge(dve_pT, NCH * b + c + 1)
                    act.activation(pr[:, c % 2, :], sc[:, c % 2, :], ACT.Exp).then_inc(act_exp, 1)
                act.wait_ge(pe_y, b + 1)
                act.activation(yS[:, :], GA[:, :], ACT.Identity).then_inc(act_y, 1)
                for n in range(4, 9):
                    beside(n)
                act.wait_ge(pe_hT, b + 1)
                act.activation(hT[:, :], GB[:, :], ACT.Identity, scale=vec[:, V_G2:V_G2 + 1],
                               bias=vec[:, V_B2:V_B2 + 1]).then_inc(act_hT, 1)
                beside(9)
                act.wait_ge(pe_mlp2, b + 1)
                for c in range(FC):
                    act.wait_ge(pe_mlp1, FC * b + c + 1)
                    act.activation(gT[:, c, :], [GA, GB, GC, GA][c][:, :], ACT.Gelu,
                                   bias=vec[:, V_M1 + c:V_M1 + c + 1]).then_inc(act_gelu, 1)
                for n in range(10, STEPS):
                    beside(n)

            def gelu(t):
                u, i = t[1] % 2, tile(t)
                act.wait_ge(pe_he, i + 1)
                need(act, pe_eo, i - 1)
                b1 = (t[1] % RING) * K_N + K_B1
                for c in range(FC):
                    ins = act.activation(heT[:, u, c * P:(c + 1) * P], S[u][:, c * P:(c + 1) * P], ACT.Gelu,
                                         bias=pk[:, b1 + c:b1 + c + 1])
                ins.then_inc(act_he, 1)

            def step(t):
                if exists(after(t, 1)):
                    gelu(after(t, 1))

            def weigh(h):
                for b in range(2 * h, 2 * h + 2):
                    act.wait_ge(gathered[b], 16 * K * TB)
                for t in range(h * T // 2, (h + 1) * T // 2):
                    ins = act.activation(comb[:, t, :], rowsk[:, 0, t, :], ACT.Identity, scale=gw[:, 0, t:t + 1])
                ins.then_inc(act_weigh, 1)

            def end(n):
                if n == 6:
                    act.wait_ge(gates, 3)
                    weigh(0)

            sequences(act, attend, step, start=start, end=end)
            weigh(1)

        @block.tensor
        def _(pe):
            pe.wait_ge(w_in, 64)

            def turn(b):
                pe.wait_ge(xh_ready, b + 1)
                for t in range(TB):
                    last = nc.tensor.transpose(XT4[b][:, t * P:(t + 1) * P],
                                               xhat[:, b * TB + t, :], ident)
                last.then_inc(pe_xT, 1)

            def route(b):
                pe.wait_ge(act_xT, b + 1)
                for t in range(TB):
                    n = b * TB + t
                    last = mm(GC[:, n * E:(n + 1) * E], xrT[:, b % 2, t * P:(t + 1) * P], rw[:, :],
                              start=True, stop=True)
                last.then_inc(pe_logit, 1)

            turn(0)
            for b in range(NB):
                if b + 1 < NB:
                    turn(b + 1)
                route(b)

            def start(n):
                if n == 0:
                    pe.wait_ge(picks_ready, 1)
                    pe.wait_ge(pool_const, 3)
                    mm(XT[:, 0:ET], const[:, C_TRI:C_TRI + P], picks, start=True, stop=True)
                    mm(EO[:, 0:ET], ones[:, :], picks, start=True, stop=True).then_inc(pe_rank, 1)

            pe.sem_inc(pe_scores, NCH)
            pe.sem_inc(pe_gate, 1)
            pe.sem_inc(pe_pv, 1)
            pe.sem_inc(pe_mlp2, 1)
            pe.wait_ge(dve_setup, 6)
            pe.wait_ge(act_xn, 1)
            pe.wait_ge(logit_read, 1)

            def bias_row(out, at):
                mm(out, sel0[:, :], rowp[:, at:at + D].unsqueeze(1).to_broadcast([RP, TB, D]),
                   start=True, stop=False, skip_group_check=True)

            def sums(out, h):
                q, k = slice(h * SEQ // 2, (h + 1) * SEQ // 2), slice(h * NBLK // 2, (h + 1) * NBLK // 2)
                for s in range(2):
                    for g in range(HG):
                        last = mm(out[g * W:(g + 1) * W, q], const[:, C_BLK:C_BLK + W], pT[:, k, g, s, :],
                                  start=(s == 0), stop=(s == 1), skip_group_check=True)
                last.then_inc(pe_den, 1)

            def per_tile(out, lhs, rhs, h=None):
                for t in range(TB) if h is None else range(h * TB // 2, (h + 1) * TB // 2):
                    last = mm(out[:, t * P:(t + 1) * P], lhs[:, t * P:(t + 1) * P], rhs, start=False,
                              stop=(t == TB - 1), skip_group_check=True)
                return last

            def pv(kb, first):
                n = 2 if kb + 1 < NBLK else 1
                lo = pT[:, kb, 0, 1, :]
                for g in range(HG):
                    rhs = bass.AP(lo.tensor, lo.offset + g * 2 * W, [list(lo.ap[0]), [HG * 2 * W - W, n], [1, W]])
                    last = mm(OV[g * W:(g + 1) * W, kb * W:(kb + n) * W], vx[:, kb, g * W:(g + 1) * W], rhs,
                              start=first, stop=(kb == NBLK - 1), skip_group_check=True)
                return last

            def attend(b, beside):
                pe.wait_ge(xa_ready, b + 1)
                pe.wait_ge(act_gelu, FC * b + 4)
                mm(GA[:, :], wqkv[:, 0:D], xa[:, :], start=True, stop=True).then_inc(pe_q, 1)
                mm(GB[:, :], wqkv[:, D:2 * D], xa[:, :], start=True, stop=True).then_inc(pe_k, 1)
                beside(0)
                mm(GC[:, :], wdrive[:, :], xa[:, :], start=True, stop=True).then_inc(pe_drive, 1)
                pe.wait_ge(act_q, b + 1)
                wv = wqkv[:, 2 * D:3 * D].rearrange("p (g m d) -> p g m d", g=HG, m=4)
                for kb in range(NBLK):
                    for m in range(4):
                        last = mm(GA[m * W:(m + 1) * W, kb * W:(kb + 1) * W], xa[:, kb * W:(kb + 1) * W],
                                  wv[:, :, m, :], start=True, stop=True)
                last.then_inc(pe_v, 1)
                pe.wait_ge(act_k, b + 1)
                bias_row(GB[:, :], R_G)
                per_tile(GB, xa, wug[:, D:2 * D]).then_inc(pe_gate, 1)
                for n in range(1, 4):
                    beside(n)

                pe.wait_ge(dve_kx, b + 2)
                pe.wait_ge(act_kx, b + 1)
                if isinstance(b, int) and b == 0:
                    pe.wait_ge(act_xn, NB - 1)
                    pe.wait_ge(wo_in, 16 * 5)
                else:
                    pe.wait_ge(act_he, NT if isinstance(b, int) else (b - 1) * STEPS + LEAD - 2 + 5)
                for c in range(NCH + 3):
                    if c < NCH:
                        pe.wait_ge(dve_sub, NCH * b + c + 1)
                        m0 = maskb[:, 0:4 * W].rearrange("p (a k) -> p a k", a=2).unsqueeze(2).to_broadcast([P, 2, HG, 2 * W]) \
                            if c == 0 else maskb[:, 2 * W:4 * W].unsqueeze(1).to_broadcast([P, 2 * HG, 2 * W])
                        mm(S[c % 2][:, :], identb[:, :], m0, start=True, stop=False, skip_group_check=True)
                        for k in range(2):
                            j = 2 * c + k
                            for m in range(4):
                                last = mm(S[c % 2][m * W:(m + 1) * W, k * 256:(k + 1) * 256],
                                          qT[:, j * W:(j + 1) * W], kx[:, m, :, j * W:(j + 2) * W],
                                          start=False, stop=(k == 1), skip_group_check=True)
                        last.then_inc(pe_scores, 1)
                    if c == 3:
                        pe.wait_ge(dve_scan, b + 2)
                        pe.wait_ge(dve_vx, b + 1)
                        for t in range(TB):
                            last = mm(GA[:, t * P:(t + 1) * P], states[:, t * P:(t + 1) * P], cw[:, :],
                                      start=True, stop=True)
                        last.then_inc(pe_y, 1)
                        pe.wait_ge(dve_acc, b + 1)
                    if c >= 3:
                        n = c - 3
                        pe.wait_ge(dve_pT, NCH * b + n + 3)
                        if n:
                            pv(2 * n - 1, False)
                        last = pv(2 * n, n == 0)
                        if n == NCH // 2:
                            pe.wait_ge(act_drive, b + 1)
                            sums(GC, 0)
                last = pv(NBLK - 1, False)
                last.then_inc(pe_pv, 1)
                pe.wait_ge(act_gate, b + 1)
                sums(GB, 1)
                pe.wait_ge(dve_sub, NCH * b + NCH + 2)
                for n in range(4, 6):
                    beside(n)
                pe.wait_ge(dve_rden, 2 * b + 1)
                bias_row(GC[:, :], R_O)
                for h in range(2):
                    pe.wait_ge(dve_oT, 2 * b + h + 1)
                    last = per_tile(GC, oT, wo[:, :], h)
                last.then_inc(pe_attn, 1)
                for n in range(6, 9):
                    beside(n)
                pe.wait_ge(dve_h, b + 1)
                for t in range(TB):
                    last = nc.tensor.transpose(GB[:, t * P:(t + 1) * P], hh[:, t * P:(t + 1) * P], ident)
                last.then_inc(pe_hT, 1)
                beside(9)
                pe.wait_ge(act_hT, b + 1)
                for c in range(FC):
                    if c == 0:
                        pe.wait_ge(act_y, b + 2)
                    if c == 2:
                        pe.wait_ge(dve_attn, b + 1)
                    if c == 3:
                        pe.wait_ge(act_gelu, FC * b + 5)
                    mm([GA, GB, GC, GA][c][:, :], m1[:, c * P:(c + 1) * P], hT[:, :], start=True, stop=True
                       ).then_inc(pe_mlp1, 1)
                beside(10)
                bias_row(OV[:, :], R_M2)
                for c in range(FC):
                    pe.wait_ge(act_gelu, FC * b + c + 5)
                    for t in range(TB):
                        last = mm(OV[:, t * P:(t + 1) * P], gT[:, c, t * P:(t + 1) * P], m2[:, c, :],
                                  start=False, stop=(c == FC - 1), skip_group_check=True)
                last.then_inc(pe_mlp2, 1)
                for n in range(11, STEPS):
                    beside(n)

            def rows_T(t):
                i, u = tile(t), t[1] % RING
                pe.wait_ge(row_in[u], 16 * turn_of(t) + 16)
                need(pe, dve_xeT, i)
                nc.tensor.transpose(XT[:, 0:P], xg[:, u, :], ident).then_inc(pe_xeT, 1)

            def layer1(t):
                i, u, w = tile(t), t[1] % 2, (t[1] % RING) * K_N + K_W1
                pe.wait_ge(dve_xeT, i + 1)
                pe.wait_ge(pk_in[t[1] % RING], 16 * turn_of(t) + 16)
                need(pe, act_he, i - 1)
                for c in range(FC):
                    last = mm(S[u][:, c * P:(c + 1) * P], pk[:, w + c * P:w + (c + 1) * P], xeT[:, u, :],
                              start=True, stop=True)
                last.then_inc(pe_he, 1)

            def layer2(t):
                i, u, w = tile(t), t[1] % 2, (t[1] % RING) * K_N + K_W2
                pe.wait_ge(act_he, i + 1)
                need(pe, dve_eo, i)
                for c in range(FC):
                    last = mm(EO[:, 0:P], heT[:, u, c * P:(c + 1) * P], pk[:, w + c * P:w + (c + 1) * P],
                              start=(c == 0), stop=(c == FC - 1))
                last.then_inc(pe_eo, 1)

            def step(t):
                for part, k in ((rows_T, 2), (layer1, 1), (layer2, 0)):
                    if exists(after(t, k)):
                        part(after(t, k))

            sequences(pe, attend, step, start=start)

        @block.vector
        def _(v):
            count = [0]
            link = chain(v, count)
            tt, ts, stt = v.tensor_tensor, v.tensor_scalar, v.scalar_tensor_tensor

            def moments(stats, out, done=dve):
                me, ve, mo, vo = (stats[:, :, n] for n in (1, 2, 4, 5))
                tt(out[:, 0, :], me, mo, ALU.add).then_inc(done, 1)
                tt(out[:, 1, :], me, mo, ALU.subtract).then_inc(done, 1)
                tt(out[:, 2, :], ve, vo, ALU.add).then_inc(done, 1)
                return 3

            v.sem_inc(dve_sub, 2)
            v.sem_inc(dve_pT, 2)
            v.sem_inc(dve_kx, 1)
            v.sem_inc(dve_scan, 1)
            v.sem_inc(dve_acc, 1)

            for b in range(NB):
                v.wait_ge(x_in[b], 16)
                for t in range(b * TB, b * TB + TB):
                    ins = v.bn_stats(st[:, t, :], x[:, t, :])
            link(ins)
            count[0] += moments(st, lnt)
            v.wait_ge(dve, count[0])
            ts(lnt[:, 0, :], lnt[:, 0, :], 0.5, None, ALU.mult).then_inc(dve, 1)
            count[0] += 1
            link(tt(lnt[:, 1, :], lnt[:, 1, :], lnt[:, 1, :], ALU.mult))
            link(stt(lnt[:, 2, :], lnt[:, 1, :], D / 4, lnt[:, 2, :], ALU.mult, ALU.add))
            link(ts(lnt[:, 3, :], lnt[:, 2, :], 1.0 / D, EPS, ALU.mult, ALU.add))
            link(v.reciprocal(lnt[:, 1, :], lnt[:, 3, :]))
            link(stt(lnt[:, 2, :], lnt[:, 2, :], 1.0 / D, lnt[:, 1, :], ALU.mult, ALU.mult))
            link(ts(lnt[:, 4, :], lnt[:, 2, :], EPS, None, ALU.add))
            a, y, w = lnt[:, 3:5, :], lnt[:, 5:7, :], lnt[:, 8:10, :]
            link(ts(w.bitcast(I32), a.bitcast(I32), 1, None, ALU.logical_shift_right))
            link(ts(y.bitcast(I32), w.bitcast(I32), -1.0, float(MAGIC), ALU.mult, ALU.add))
            for _ in range(3):
                link(tt(w, y, y, ALU.mult))
                link(stt(w, w, -0.5, a, ALU.mult, ALU.mult))
                link(stt(y, w, 1.5, y, ALU.add, ALU.mult))
            tt(lnt[:, 7, :], lnt[:, 5, :], lnt[:, 6, :], ALU.mult).then_inc(dve, 1)
            count[0] += 1
            stt(lnt[:, 10, :], lnt[:, 0, :], -1.0, lnt[:, 5, :], ALU.mult, ALU.mult).then_inc(nmr_ready, 1)
            v.wait_ge(dve, count[0])

            for b in range(NB):
                for t in range(TB * b, TB * b + TB):
                    ins = ts(xhat[:, t, :], x[:, t, :], lnt[:, 0, t:t + 1], lnt[:, 7, t:t + 1], ALU.subtract, ALU.mult)
                ins.then_inc(xh_ready, 1)

            v.wait_ge(w_in, 64)
            v.wait_ge(wm_in, 64)
            tt(wdrive[:, :], bw[:, :], wug[:, 0:D], ALU.add).then_inc(dve_setup, 1)
            v.tensor_copy(identb[:, :], ident).then_inc(dve_setup, 1)
            v.tensor_copy(maskb[:, :], const[:, C_MASK:C_MASK + 4 * W]).then_inc(dve_setup, 1)
            link(tt(rowf[:, R_M2:R_M2 + D], rowf[:, R_M2:R_M2 + D], rowf[:, R_OB:R_OB + D], ALU.add))
            link(v.tensor_copy(rowp[:, :], rowf))
            link(tt(rowf, rowf, rowp[:, :], ALU.subtract))
            v.tensor_copy(rowp[QR:2 * QR, :], rowf[QR:2 * QR]).then_inc(dve_setup, 1)
            link(v.tensor_copy(rowp[2 * QR:RP, :], rowf[2 * QR:RP]))
            link(tt(rowf[2 * QR:RP], rowf[2 * QR:RP], rowp[2 * QR:RP, :], ALU.subtract))
            v.tensor_copy(rowp[2 * QR:RP, :], rowf[2 * QR:RP]).then_inc(dve_setup, 1)
            v.wait_ge(pool_const, 3)
            ts(sel0[:, :], ones[0:RP, :], const[0:RP, C_SEL:C_SEL + 1], None, ALU.mult).then_inc(dve_setup, 1)

            v.wait_ge(pe_logit, NB)
            link(tt(logit[:, :, :], GC[:, 0:T * E].rearrange("p (t e) -> p t e", e=E),
                    rb[:, :].unsqueeze(1).to_broadcast([P, T, E]), ALU.add))
            v.sem_inc(logit_read, 1)
            for t in range(T):
                ins = v.max(top[:, t, :], logit[:, t, :])
            link(ins)
            for t in range(T):
                ins = v.max_index(topi[:, t, :], top[:, t, :], logit[:, t, :])
            link(ins)
            link(v.tensor_copy(topf[:, :, :].rearrange("p k t -> p t k"), topi[:, :, 0:K]))
            for k in range(K):
                ins = tt(pick[:, k, :, :], topf[:, k, :].unsqueeze(1).to_broadcast([P, E, T]),
                         const[:, C_IE:C_IE + E].unsqueeze(2).to_broadcast([P, E, T]), ALU.is_equal)
            link(ins)
            tt(picks[:, :].rearrange("p (e t) -> p e t", e=E), pick[:, 0, :, :], pick[:, 1, :, :], ALU.add
               ).then_inc(picks_ready, 1)
            tt(gw[:, 3, :], top[:, :, 1], top[:, :, 0], ALU.subtract).then_inc(diff_ready, 1)
            v.wait_ge(pe_rank, 1)
            link(v.tensor_copy(tot[:, :], EO[:, 0:E * T]))
            link(v.tensor_tensor_scan(incl[:, :], const[:, C_RESET:C_RESET + E * T], tot[:, :], 0.0, ALU.mult, ALU.add))
            incl3 = incl[:, :].rearrange("p (e t) -> p e t", e=E)
            link(tt(cmpj[:, :, :], incl3[:, :, T - 1:T].to_broadcast([P, E, MB]),
                    const[:, C_J:C_J + MB].unsqueeze(1).to_broadcast([P, E, MB]), ALU.is_gt))
            link(v.tensor_reduce(blocks[:, 0, :], cmpj[:, :, :], AX_X, ALU.add))
            link(v.tensor_tensor_scan(blocks[:, 1, :], const[:, C_ONE:C_ONE + E], blocks[:, 0, :], 0.0, ALU.mult, ALU.add))
            link(tt(blocks[:, 2, :], blocks[:, 1, :], blocks[:, 0, :], ALU.subtract))
            link(ts(blocks[:, 3, :], blocks[:, 2, :], float(P), None, ALU.mult))
            link(tt(base[:, :], incl[:, :], tot[:, :], ALU.subtract))
            link(tt(base[:, :], base[:, :], XT[:, 0:E * T], ALU.add))
            link(tt(base[:, :].rearrange("p (e t) -> p e t", e=E), base[:, :].rearrange("p (e t) -> p e t", e=E),
                    blocks[:, 3, :].unsqueeze(2).to_broadcast([P, E, T]), ALU.add))
            for k in range(K):
                ins = tt(slotf[:, k, :, :], pick[:, k, :, :], base[:, :].rearrange("p (e t) -> p e t", e=E), ALU.mult)
            link(ins)
            for k in range(K):
                ins = v.tensor_reduce(slots[:, k, :], slotf[:, k, :, :].rearrange("p e t -> p t e"), AX_X, ALU.add)
            link(ins)
            v.tensor_copy(sloti[:, :, :], slots[:, :, :]).then_inc(slots_ready, 1)

            link(tt(tcmp[:, :, :], const[0:1, C_TI:C_TI + NT].unsqueeze(2).to_broadcast([1, NT, E]),
                    blocks[0:1, 1, :].unsqueeze(1).to_broadcast([1, NT, E]), ALU.is_ge))
            link(v.tensor_reduce(texpf[:, 0, :], tcmp[:, :, :], AX_X, ALU.add))
            link(ts(texpf[:, 1, :], texpf[:, 0, :], float(E - 1), None, ALU.min))
            v.tensor_copy(texp[:, :], texpf[:, 1, :]).then_inc(texp_ready, 1)

            def start(n):
                if n == 4:
                    v.wait_ge(diff_exp, 1)
                    ts(gw[:, 3, :], gw[:, 2, :], 1.0, None, ALU.add).then_inc(gates, 1)
                    v.wait_ge(gates, 1)
                    v.reciprocal(gw[:, 0, :], gw[:, 3, :]).then_inc(gates, 1)
                    v.wait_ge(gates, 2)
                    tt(gw[:, 1, :], gw[:, 2, :], gw[:, 0, :], ALU.mult).then_inc(gates, 1)

            CH = 11
            k0 = count[0]

            def attend(b, beside):
                n = [0]

                def link1(ins):
                    n[0] += 1
                    ins.then_inc(dve, 1)
                    v.wait_ge(dve, b * CH + k0 + n[0])

                v.wait_ge(act_k, b + 1)
                v.wait_ge(pe_scores, NCH * b + NCH)
                beside(0)
                for i, (m, g) in enumerate(spread(b)[0]):
                    if i == 8:
                        beside(1)
                    ins = ts(kx[:, m, g, W:], kT[:, :], const[:, C_HEAD + 4 * g + m:C_HEAD + 4 * g + m + 1],
                             None, ALU.mult)
                ins.then_inc(dve_kx, 1)
                beside(2)
                v.wait_ge(pe_pv, b + 1)
                v.wait_ge(pe_v, b + 1)
                tt(vx[:, :, :].rearrange("p k (g m d) -> p (k g) m d", g=HG, m=4),
                   GA[:, :].rearrange("p (n d) -> p n d", d=DH).unsqueeze(2).to_broadcast([P, NBLK * HG, 4, DH]),
                   const[:, C_BLK:C_BLK + W].rearrange("p (m d) -> p m d", m=4).unsqueeze(1).to_broadcast(
                       [P, NBLK * HG, 4, DH]), ALU.mult).then_inc(dve_vx, 1)
                beside(3)
                v.wait_ge(act_drive, b + 1)
                v.tensor_tensor_scan(states[:, :], vec[:, V_A:V_A + 1].to_broadcast([P, SEQ]), drive[:, :], 0.0,
                                     ALU.mult, ALU.add).then_inc(dve_scan, 1)
                for c in range(NCH + 1):
                    if c < NCH:
                        s3 = S[c % 2][:, :].rearrange("p (u k) -> p u k", u=8)
                        v.wait_ge(pe_scores, NCH * b + NCH + c + 1)
                        v.tensor_reduce(smax[:, c % 2, :], s3, AX_X, ALU.max).then_inc(dve_max, 1)
                        v.wait_ge(dve_max, NCH * b + c + 1)
                        if c >= 2:
                            v.wait_ge(act_exp, NCH * b + c - 1)
                        tt(sc[:, c % 2, :].rearrange("p (u k) -> p u k", u=8), s3,
                           smax[:, c % 2, :].unsqueeze(2).to_broadcast([P, 8, 2 * W]), ALU.subtract
                           ).then_inc(dve_sub, 1)
                    if c >= 1:
                        i = c - 1
                        v.wait_ge(act_exp, NCH * b + i + 1)
                        v.transpose(pT[:, 2 * i:2 * i + 2, :, :, :].rearrange("p a g s q -> p (a g s q)"),
                                    pr[:, i % 2, :]).then_inc(dve_pT, 1)
                for h in range(2):
                    q = slice(h * SEQ // 2, (h + 1) * SEQ // 2)
                    v.wait_ge(pe_den, 2 * b + h + 1)
                    v.reciprocal(rden[:, q], [GC, GB][h][:, q]).then_inc(dve_rden, 1)
                    v.wait_ge(dve_rden, 2 * b + h + 1)
                    v.wait_ge(pe_pv, b + 2)
                    tt(oT[:, q], OV[:, q], rden[:, q], ALU.mult).then_inc(dve_oT, 1)
                    if h == 0:
                        beside(4)
                v.wait_ge(act_y, b + 2)
                v.wait_ge(norm1, 2)
                link1(tt(mix[:, 0, :], yS[:, :], xn[:, bass.ds(b * TB, TB), :].rearrange("p t d -> p (t d)"), ALU.add))
                beside(5)
                v.wait_ge(pe_attn, b + 1)
                tt(mix[:, 1, :], GC[:, :], yS[:, :], ALU.subtract).then_inc(dve_attn, 1)
                v.wait_ge(dve_attn, b + 1)
                v.wait_ge(act_gate, b + 1)
                link1(stt(mix[:, 2, :], gate[:, :], 1.0, mix[:, 1, :], ALU.add, ALU.mult))
                link1(stt(x2[:, :], mix[:, 2, :], 0.5, mix[:, 0, :], ALU.mult, ALU.add))
                beside(6)
                for t in range(TB):
                    ins = v.bn_stats(st2[:, t, :], x2[:, t * D:(t + 1) * D])
                link1(ins)
                n[0] += moments(st2, ln2)
                v.wait_ge(dve, b * CH + k0 + n[0])
                link1(ts(ln2[:, 0, :], ln2[:, 0, :], 0.5, None, ALU.mult))
                link1(tt(ln2[:, 1, :], ln2[:, 1, :], ln2[:, 1, :], ALU.mult))
                link1(stt(ln2[:, 2, :], ln2[:, 1, :], D / 4, ln2[:, 2, :], ALU.mult, ALU.add))
                ts(ln2[:, 3, :], ln2[:, 2, :], 1.0 / D, EPS, ALU.mult, ALU.add).then_inc(var_ready, 1)
                if not (isinstance(b, int) and b == NB - 1):
                    v.wait_ge(pe_gate, b + 2)
                    v.tensor_copy(xa[:, :], xn1T[:, bass.ds((b + 1) * SEQ, SEQ)]).then_inc(xa_ready, 1)
                beside(7)
                v.wait_ge(rstd_ready, b + 1)
                for t in range(TB):
                    ins = ts(hh[:, t * D:(t + 1) * D], x2[:, t * D:(t + 1) * D], ln2[:, 0, t:t + 1],
                             ln2[:, 4, t:t + 1], ALU.subtract, ALU.mult)
                ins.then_inc(dve_h, 1)
                beside(8)
                link1(tt(mix[:, 0, :], x2[:, :], x[:, bass.ds(b * TB, TB), :].rearrange("p t d -> p (t d)"), ALU.add))
                for k in range(9, 11):
                    beside(k)
                v.wait_ge(pe_mlp2, b + 2)
                v.wait_ge(scattered, 16 * K * T)
                tt(acc[:, bass.ds(b * TB, TB), :].rearrange("p t d -> p (t d)"), OV[:, :], mix[:, 0, :], ALU.add
                   ).then_inc(dve_acc, 1)
                for k in range(11, STEPS):
                    beside(k)
                assert n[0] == CH, n[0]

            def rows_T(t):
                i, u, w = tile(t), t[1] % 2, (t[1] % RING) * K_N
                v.wait_ge(pe_xeT, i + 1)
                v.wait_ge(pk_in[t[1] % RING], 16 * turn_of(t) + 16)
                need(v, pe_he, i - 1)
                ts(xeT[:, u, :], XT[:, 0:P], pk[:, w + K_EW:w + K_EW + 1], pk[:, w + K_EB:w + K_EB + 1],
                   ALU.mult, ALU.add).then_inc(dve_xeT, 1)

            def finish(t):
                i, u, w = tile(t), t[1] % RING, (t[1] % RING) * K_N + K_B2
                v.wait_ge(pe_eo, i + 1)
                need(v, row_out[u], 16 * turn_of(t))
                tt(eo[:, u, :], EO[:, 0:P], pk[:, w:w + D], ALU.add).then_inc(dve_eo, 1)

            def step(t):
                for part, k in ((rows_T, 2), (finish, 0)):
                    if exists(after(t, k)):
                        part(after(t, k))

            C3 = 9
            HT2 = T // 2

            def combine(h):
                n = [h * C3]
                tiles = range(h * HT2, (h + 1) * HT2)

                def link3(ins):
                    n[0] += 1
                    ins.then_inc(comb_chain, 1)
                    v.wait_ge(comb_chain, n[0])

                v.wait_ge(act_weigh, h + 1)
                for t in tiles:
                    ins = stt(comb[:, t, :], rowsk[:, 1, t, :], gw[:, 1, t:t + 1], comb[:, t, :], ALU.mult, ALU.add)
                link3(ins)
                for t in tiles:
                    ins = v.bn_stats(st3[:, t % HT2, :], comb[:, t, :])
                link3(ins)
                moments(st3, ln3, comb_chain)
                n[0] += 3
                v.wait_ge(comb_chain, n[0])
                link3(ts(ln3[:, 0, :], ln3[:, 0, :], 0.5, None, ALU.mult))
                link3(tt(ln3[:, 1, :], ln3[:, 1, :], ln3[:, 1, :], ALU.mult))
                link3(stt(ln3[:, 2, :], ln3[:, 1, :], D / 4, ln3[:, 2, :], ALU.mult, ALU.add))
                if h:
                    v.wait_ge(rstd3_ready, h)
                ts(ln3[:, 3, :], ln3[:, 2, :], 1.0 / D, EPS, ALU.mult, ALU.add).then_inc(var3_ready, 1)
                for t in tiles:
                    ins = stt(comb[:, t, :], comb[:, t, :], ln3[:, 0, t % HT2:t % HT2 + 1], ow[:, :],
                              ALU.subtract, ALU.mult)
                link3(ins)

            def out(h):
                v.wait_ge(rstd3_ready, h + 1)
                for b in range(2 * h, 2 * h + 2):
                    for t in range(b * TB, b * TB + TB):
                        ins = stt(comb[:, t, :], comb[:, t, :], rstd3[:, t:t + 1], acc[:, t, :], ALU.mult, ALU.add)
                    ins.then_inc(out_ready, 1)

            def end(n):
                if n == 9:
                    combine(0)

            sequences(v, attend, step, start=start, end=end)
            combine(1)
            out(0)
            out(1)


def kernel(**inputs):
    import concourse.bacc as _bacc
    from concourse.bass_utils import run_bass_kernel_spmd as _run

    a = {k: np.ascontiguousarray(v) for k, v in inputs.items()}

    def at(n):
        return a["L0_attn_" + n]

    def ft(n):
        return a["L0_ffn_" + n]

    bug = at("b_ug")
    vec = np.concatenate(
        [np.stack([at("ln1_g"), at("ln1_b"), at("ln2_g"), at("ln2_b"), bug[:D], at("A"), ft("router_ln_w"),
                   ft("router_ln_b")]), at("mlp_b1").reshape(FC, P)]).T
    row = np.zeros((3, QR, R_N), np.float32)
    for at_, n in ((R_G, bug[D:]), (R_O, at("b_O")), (R_M2, at("mlp_b2")), (R_OB, ft("out_ln_b"))):
        row[:, 0, at_:at_ + D] = n
    pk = np.concatenate(
        [ft("w1"), ft("w2").reshape(E, FC, P, D).transpose(0, 2, 1, 3).reshape(E, P, FC * D),
         ft("exp_ln_w")[:, :, None], ft("exp_ln_b")[:, :, None], ft("b1").reshape(E, FC, P).transpose(0, 2, 1),
         np.broadcast_to(ft("b2")[:, None, :], (E, P, D))], axis=2)
    arrays = {
        "x": at("x"), "const": constants(), "vec": np.ascontiguousarray(vec), "row": row.reshape(RP, R_N),
        "wqkv": at("W_qkv"), "wo": at("W_O"), "wug": at("W_ug"), "bw": at("B_w"), "cw": at("C_w"),
        "m1": at("mlp_W1"), "m2": at("mlp_W2"), "rw": ft("router_w"), "rb": ft("router_b"), "pk": np.ascontiguousarray(pk),
        "ow": ft("out_ln_w"),
    }
    nc = _bacc.Bacc("TRN2", target_bir_lowering=False, num_devices=1)
    args = [nc.dram_tensor(f"in_{n}", v.shape, mybir.dt.from_np(v.dtype), kind="ExternalInput").ap()
            for n, v in arrays.items()]
    out = nc.dram_tensor("out_0", (NB, SEQ, D), F32, kind="ExternalOutput").ap()
    program(nc, *args, out)
    r = _run(nc, [{f"in_{n}": v for n, v in arrays.items()}], core_ids=[0])
    return r.results[0]["out_0"]
```

```python
from contextlib import ExitStack

import numpy as np

import concourse.bass as bass
from concourse import mybir

ALU = mybir.AluOpType
ACT = mybir.ActivationFunctionType
F32 = mybir.dt.float32
BF16 = mybir.dt.bfloat16
I32 = mybir.dt.int32
U32 = mybir.dt.uint32
AX_X = mybir.AxisListType.X

P = 128
D = 128
NB, SEQ = 4, 512
T = NB * SEQ // P
TB = SEQ // P
H, DH = 16, 8
HG = 4
W = 32
NBLK = SEQ // W
NCH = NBLK // 2
E, FF, K = 8, 512, 2
FC = FF // P
NT = (NB * SEQ * K) // P + E - 1
MB = NB * SEQ // P
EPS = 1e-5
NEG = -1e30

C_ID = 0
C_TRI = C_ID + P
C_HEAD = C_TRI + P
C_BLK = C_HEAD + H
C_MASK = C_BLK + W
C_RESET = C_MASK + 4 * W
C_IE = C_RESET + E * T
C_J = C_IE + E
C_TI = C_J + MB
C_SEL = C_TI + NT
C_ONE = C_SEL + 1
C_ID0 = C_ONE + E
C_PAD = C_ID0 + K * T
C_N = C_PAD + NT
V_G1, V_B1, V_G2, V_B2, V_BU, V_A, V_RW, V_RB = range(8)
V_M1 = 8
V_N = V_M1 + FC
K_W1 = 0
K_W2 = K_W1 + FF
K_EW = K_W2 + FC * D
K_EB = K_EW + 1
K_B1 = K_EB + 1
K_B2 = K_B1 + FC
K_N = K_B2 + D
R_G, R_O, R_M2, R_OB = 0, D, 2 * D, 3 * D
R_N = 4 * D
QR = 32
RP = 3 * QR
RING = 6
STEPS = 12
LEAD = 10
DRAIN = NT - (LEAD - 2) - (NB - 2) * STEPS
DR = D + 1
MAGIC = 0x5F3759DF


def constants():
    c = np.zeros((P, C_N), np.float32)
    p = np.arange(P)
    c[:, C_ID:C_ID + P] = np.eye(P)
    c[:, C_TRI:C_TRI + P] = p[:, None] < p[None, :]
    c[:, C_HEAD:C_HEAD + H] = p[:, None] // DH == np.arange(H)[None, :]
    c[:, C_BLK:C_BLK + W] = p[:, None] // W == np.arange(W)[None, :] // DH
    q, k = p[:, None] % W, np.arange(2 * W)[None, :]
    band = (k > q) & (k <= q + W)
    c[:, C_MASK:C_MASK + 2 * W] = np.where(band & (k >= W), 0.0, NEG)
    c[:, C_MASK + 2 * W:C_MASK + 4 * W] = np.where(band, 0.0, NEG)
    c[:, C_RESET:C_RESET + E * T] = np.arange(E * T)[None, :] % T != 0
    c[:, C_IE:C_IE + E] = np.arange(E)
    c[:, C_J:C_J + MB] = np.arange(MB) * P
    c[:, C_TI:C_TI + NT] = np.arange(NT)
    c[:, C_ONE:C_ONE + E] = 1.0
    c[:, C_SEL] = p % QR == 0
    for n in range(K * T):
        c[:, C_ID0 + n] = n * P + p
    for n in range(NT):
        c[:, C_PAD + n] = (K * T + n) * P + p
    return c


def program(nc, x_d, const_d, vec_d, row_d, wqkv_d, wo_d, wug_d, bw_d, cw_d, m1_d, m2_d,
            rw_d, rb_d, pk_d, ow_d, out_d):
    xs_d = nc.dram_tensor("sorted_rows", (NT * P, DR), F32).ap()
    es_d = nc.dram_tensor("expert_rows", ((K * T + NT) * P, D), F32).ap()
    mm = nc.tensor.matmul
    ctx = ExitStack()
    with ctx:
        def sb(name, shape, dt=F32):
            return ctx.enter_context(nc.sbuf_tensor(name, shape, dt))

        def bank(name):
            return ctx.enter_context(nc.psum_tensor(name, [P, 512], F32))

        def sem(name):
            return ctx.enter_context(nc.semaphore(name))

        const = sb("const", [P, C_N])
        vec = sb("vec", [P, V_N])
        rowp = sb("rowp", [RP, R_N], BF16)
        sel0 = sb("sel0", [RP, P], BF16)
        wqkv = sb("wqkv", [P, 3 * D])
        wo = sb("wo", [P, D])
        wug = sb("wug", [P, 2 * D])
        bw = sb("bw", [P, D])
        cw = sb("cw", [P, D])
        m1 = sb("m1", [P, FF])
        m2 = sb("m2", [P, FC, D])
        rw = sb("rw", [P, W])
        rb = sb("rb", [P, E])
        ow = sb("ow", [P, D])
        wdrive = sb("wdrive", [P, D])
        wv = sb("wv", [P, D])
        identb = sb("identb", [P, P], BF16)
        maskb = sb("maskb", [P, 4 * W], BF16)
        ones = sb("ones", [P, P])
        power = sb("power", [P, T // 2])
        ident = const[:, C_ID:C_ID + P]

        x = sb("x", [P, T, D])
        xn = sb("xn", [P, T, D])
        xrow = sb("xrow", [P, T, DR])
        xhat = xrow[:, :, 0:D]
        xn1T = sb("xn1T", [P, T * P])
        acc = xhat

        st = sb("st", [P, T, 6])
        lnt = sb("lnt", [P, 12, T])
        topf = sb("topf", [P, K, T])
        gw = sb("gw", [P, 4, T])
        blocks = sb("blocks", [P, 4, E])
        slots = sb("slots", [P, K, T])
        sloti = sb("sloti", [P, K, T], I32)
        tcmp = sb("tcmp", [1, NT, E])
        texpf = sb("texpf", [1, 2, NT])
        texp = sb("texp", [1, NT], I32)

        xa = sb("xa", [P, SEQ])
        qT = sb("qT", [P, SEQ])
        kT = sb("kT", [P, SEQ])
        kx = sb("kx", [P, 4, HG, W + SEQ])
        vx = sb("vx", [P, NBLK, D])
        vT = sb("vT", [P, SEQ])
        drive = sb("drive", [P, SEQ])
        states = sb("states", [P, SEQ])
        gate = sb("gate", [P, SEQ])
        smax = sb("smax", [P, 2, 8])
        sc = sb("sc", [P, 2, 512])
        pr = sb("pr", [P, 2, 512])
        xrT = pr
        pT = sb("pT", [P, NBLK, HG, 2, W])
        rden = sb("rden", [P, SEQ])
        oT = sb("oT", [P, SEQ])
        yS = sb("yS", [P, SEQ])
        xy = sb("xy", [P, SEQ])
        mix = sb("mix", [P, 3, SEQ])
        x2 = sb("x2", [P, SEQ])
        spare = sb("spare", [P, 1])
        st2 = sb("st2", [P, TB, 6])
        ln2 = sb("ln2", [P, 8, TB])
        hh = sb("hh", [P, SEQ])
        hT = sb("hT", [P, SEQ])
        gT = sb("gT", [P, FC, SEQ])
        rowf = sc[0:RP, 0, 0:R_N]
        ET = E * T
        early = gT[:, :, :].rearrange("p c n -> p (c n)")
        logit = early[:, 0:ET].rearrange("p (t e) -> p t e", e=E)
        top = early[:, ET:2 * ET].rearrange("p (t e) -> p t e", e=8)
        topi = early[:, 2 * ET:3 * ET].bitcast(U32).rearrange("p (t e) -> p t e", e=8)
        pick = early[:, 3 * ET:5 * ET].rearrange("p (k e t) -> p k e t", k=K, e=E)
        picks, tot, incl, base = (early[:, n * ET:(n + 1) * ET] for n in range(5, 9))
        slotf = early[:, 9 * ET:11 * ET].rearrange("p (k e t) -> p k e t", k=K, e=E)
        logitq = vT[:, :]
        cmpj = early[:, 11 * ET:11 * ET + E * MB].rearrange("p (e j) -> p e j", e=E)

        xg = sb("xg", [P, RING, DR])
        ids = sb("ids", [P, RING], I32)
        pk = sb("pk", [P, RING * K_N])
        xeT = sb("xeT", [P, 2, P])
        heT = sb("heT", [P, 2, FF])
        eo = sb("eo", [P, RING, D])

        rowsk = pk[:, 0:K * T * D].rearrange("p (k t d) -> p k t d", k=K, t=T)
        comb = sb("comb", [P, T, D])
        padding = pk[:, 0:NT * DR].rearrange("p (n d) -> p n d", d=DR)
        st3 = sb("st3", [P, T // 2, 6])
        ln3 = sb("ln3", [P, 4, T // 2])
        rstd3 = sb("rstd3", [P, T])

        GA, GB, GC = bank("GA"), bank("GB"), bank("GC")
        S = [bank("S0"), bank("S1")]
        OV, XT, EO = bank("OV"), bank("XT"), bank("EO")
        XT4 = [GA, GB, S[0], S[1]]

        x_in = [sem(f"x_in{b}") for b in range(NB)]
        w_in = sem("w_in")
        wm_in = sem("wm_in")
        wo_in = sem("wo_in")
        xs_zero = sem("xs_zero")
        zero_set = sem("zero_set")
        rw_set = sem("rw_set")
        pool_ids = sem("pool_ids")
        xy_ready = sem("xy_ready")
        row_ids = sem("row_ids")
        scattered = [sem("scattered0"), sem("scattered1")]
        row_in = [sem(f"row_in{n}") for n in range(RING)]
        pk_in = [sem(f"pk_in{n}") for n in range(RING)]
        row_out = [sem(f"row_out{n}") for n in range(RING)]
        gathered = [sem(f"gathered{b}") for b in range(NB)]
        texp_ready = sem("texp_ready")
        stored = sem("stored")
        pool_const = sem("pool_const")
        xa_ready = sem("xa_ready")
        dve = sem("dve_chain")
        comb_chain = sem("comb_chain")
        pool_setup = sem("pool_setup")
        xh_ready = sem("xh_ready")
        pe_xT = sem("pe_xT")
        act_xT = sem("act_xT")
        act_xn = sem("act_xn")
        nmr_ready = sem("nmr_ready")
        norm1 = sem("norm1")
        act_weigh = sem("act_weigh")
        act_warm = sem("act_warm")
        scaled3 = sem("scaled3")
        pool_weigh = sem("pool_weigh")
        pool_w3 = sem("pool_w3")
        gates = sem("gates")
        logit_read = sem("logit_read")
        pe_logit = sem("pe_logit")
        diff_ready = sem("diff_ready")
        diff_exp = sem("diff_exp")
        picks_ready = sem("picks_ready")
        pe_rank = sem("pe_rank")
        slots_ready = sem("slots_ready")
        pe_q, pe_k, pe_drive, pe_v, pe_gate = sem("pe_q"), sem("pe_k"), sem("pe_drive"), sem("pe_v"), sem("pe_gate")
        pe_scores, pe_pv, pe_den, pe_y, pe_attn = sem("pe_scores"), sem("pe_pv"), sem("pe_den"), sem("pe_y"), sem("pe_attn")
        pe_hT, pe_mlp1, pe_mlp2 = sem("pe_hT"), sem("pe_mlp1"), sem("pe_mlp2")
        act_q, act_k, act_kx, act_drive, act_gate = sem("act_q"), sem("act_k"), sem("act_kx"), sem("act_drive"), sem("act_gate")
        act_exp, act_y, act_hT, act_gelu = sem("act_exp"), sem("act_y"), sem("act_hT"), sem("act_gelu")
        dve_kx, dve_vx, dve_scan, dve_max = sem("dve_kx"), sem("dve_vx"), sem("dve_scan"), sem("dve_max")
        dve_sub, dve_pT, dve_rden, dve_oT = sem("dve_sub"), sem("dve_pT"), sem("dve_rden"), sem("dve_oT")
        dve_attn, dve_h, dve_acc = sem("dve_attn"), sem("dve_h"), sem("dve_acc")
        var_ready, rstd_ready = sem("var_ready"), sem("rstd_ready")
        pe_xeT, act_xeT, pe_he, act_he, pe_eo, dve_eo = (
            sem("pe_xeT"), sem("act_xeT"), sem("pe_he"), sem("act_he"), sem("pe_eo"), sem("dve_eo"))
        var3_ready, rstd3_ready, out_ready = sem("var3_ready"), sem("rstd3_ready"), sem("out_ready")
        out0_ready = sem("out0_ready")

        block = ctx.enter_context(nc.Block())

        def tok3(ap):
            return ap.rearrange("p (t d) -> p t d", d=D)

        def chain(eng, count):
            def link(ins):
                count[0] += 1
                ins.then_inc(dve, 1)
                eng.wait_ge(dve, count[0])
            return link

        def after(t, k):
            return t[0], t[1] + k

        def tile(t):
            return t[0] * RING + t[1]

        def turn_of(t):
            return t[0] + t[1] // RING

        def exists(t):
            return not isinstance(t[0], int) or 0 <= tile(t) < NT

        def need(eng, semaphore, value):
            if not isinstance(value, int) or value > 0:
                eng.wait_ge(semaphore, value)

        def spread(b):
            heads = [(m, g) for m in range(4) for g in range(HG)]
            n = 6 if isinstance(b, int) and b == 0 else 11
            return heads[:n], heads[n:]

        def before(n):
            return min(DRAIN, 2 * n if n <= 3 else n + 3)

        def sequences(eng, attend, step, start=lambda n: None, end=lambda n: None, unroll=False):
            first = LEAD - 2

            def lead(n):
                start(n)
                late = n - (STEPS - 2)
                if late >= 0:
                    for s in range(late, late + 1 if n < STEPS - 1 else LEAD):
                        step((0, s - 2))

            attend(0, lead)
            if unroll:
                for b in range(1, NB - 1):
                    attend(b, lambda n: step((0, (b - 1) * STEPS + first + n)))
            else:
                with eng.Fori(1, NB - 1) as b:
                    attend(b, lambda n: step(((b - 1) * (STEPS // RING), first + n)))

            def last(n):
                for s in range(before(n), before(n + 1)):
                    step((0, NT - DRAIN + s))
                end(n)

            attend(NB - 1, last)

        @block.sync
        def _(sp):
            for b in range(NB):
                sp.dma_start(x[:, b * TB:(b + 1) * TB, :], x_d[b].rearrange("(t p) d -> p t d", p=P)
                             ).then_inc(x_in[b], 16)
            for dst, src in ((const[:, :], const_d), (vec[:, :], vec_d), (rw[:, 0:E], rw_d),
                             (rb[:, :], rb_d.unsqueeze(0).to_broadcast([P, E]))):
                sp.dma_start(dst, src).then_inc(w_in, 16)
            for dst, src in ((wqkv[:, :], wqkv_d), (wug[:, :], wug_d), (bw[:, :], bw_d), (rowf, row_d)):
                sp.dma_start(dst, src).then_inc(wm_in, 16)
            for dst, src in ((wo[:, :], wo_d), (cw[:, :], cw_d), (m1[:, :], m1_d),
                             (m2[:, :, :], m2_d.rearrange("(c p) d -> p c d", p=P)),
                             (ow[:, :], ow_d.unsqueeze(0).to_broadcast([P, D]))):
                sp.dma_start(dst, src).then_inc(wo_in, 16)
            sp.wait_ge(zero_set, 2)
            sp.dma_start(xs_d.rearrange("(n p) d -> p n d", p=P), padding).then_inc(xs_zero, 16)

            def load_packet(t):
                u = t[1] % RING
                need(sp, dve_eo, tile(t) - RING + 1)
                e = sp.value_load(texp[0:1, bass.ds(tile(t), 1)], min_val=0, max_val=E - 1)
                sp.dma_start(pk[:, u * K_N:(u + 1) * K_N], pk_d[bass.ds(e, 1)].rearrange("a p n -> p (a n)")
                             ).then_inc(pk_in[u], 16)

            def load_rows(t):
                u = t[1] % RING
                need(sp, pe_xeT, tile(t) - RING + 1)
                need(sp, pool_ids, tile(t) - RING + 1)
                sp.dma_start(xg[:, u, :], xs_d[bass.ds(tile(t) * P, P), :]).then_inc(row_in[u], 16)

            sp.wait_ge(xs_zero, 16)
            sp.wait_ge(texp_ready, 1)
            for n in range(RING):
                load_packet((0, n))
            for h in range(2):
                sp.wait_ge(scattered[h], 16 * K * T // 2)
            for n in range(RING):
                load_rows((0, n))
            laps = (NT - RING) // RING
            with sp.Fori(0, laps) as j:
                for u in range(RING):
                    load_rows((j, u + RING))
                    load_packet((j, u + RING))
            for n in range((laps + 1) * RING, NT):
                load_rows((0, n))
                load_packet((0, n))
            for u in range(RING):
                sp.wait_ge(row_out[u], 16 * ((NT - 1 - u) // RING + 1))
            for b in range(NB):
                for k in range(K):
                    sp.dma_start(rowsk[:, k, b * TB:(b + 1) * TB, :],
                                 es_d[bass.ds((k * T + b * TB) * P, TB * P), :].rearrange(
                                     "(t p) d -> p t d", p=P)).then_inc(gathered[b], 16)

            def put(tiles):
                sp.dma_start(out_d.rearrange("b (t p) d -> p (b t) d", p=P)[:, tiles, :], comb[:, tiles, :]
                             ).then_inc(stored, 16)

            sp.wait_ge(out_ready, 1)
            put(slice(T // 2, T // 2 + TB))
            sp.wait_ge(out0_ready, 1)
            put(slice(0, T // 2))
            sp.wait_ge(out_ready, 2)
            put(slice(T // 2 + TB, T))
            sp.wait_ge(stored, 16 * (NB - 1))

        @block.gpsimd
        def _(pool):
            pool.memset(rw[:, E:W], 0.0).then_inc(rw_set, 1)
            pool.memset(power[:, :], -0.5).then_inc(pool_const, 1)
            pool.memset(ones[:, :], 1.0).then_inc(pool_const, 1)
            pool.memset(kx[:, :, :, 0:W], 0.0).then_inc(pool_const, 1)
            pool.wait_ge(pool_const, 3)
            pool.memset(padding[:, :, 0:D], 0.0).then_inc(zero_set, 1)
            pool.wait_ge(w_in, 64)
            pool.tensor_copy(padding[:, :, D:DR].rearrange("p n d -> p (n d)").bitcast(I32),
                             const[:, C_PAD:C_PAD + NT]).then_inc(zero_set, 1)
            pool.wait_ge(wm_in, 64)
            pool.tensor_tensor(wdrive[:, :], bw[:, :], wug[:, 0:D], ALU.add).then_inc(pool_setup, 1)
            pool.tensor_copy(wv[:, :].rearrange("p (m g d) -> p m g d", m=4, g=HG),
                             wqkv[:, 2 * D:3 * D].rearrange("p (g m d) -> p m g d", g=HG, m=4)
                             ).then_inc(pool_setup, 1)
            pool.tensor_copy(identb[:, :], ident).then_inc(pool_setup, 1)
            pool.tensor_copy(maskb[:, :], const[:, C_MASK:C_MASK + 4 * W]).then_inc(pool_setup, 1)
            pool.tensor_tensor(sel0[:, :], ones[0:RP, :], const[0:RP, C_SEL:C_SEL + 1].to_broadcast([RP, P]),
                               ALU.mult).then_inc(pool_setup, 1)
            pool.tensor_tensor(rowf[:, R_M2:R_M2 + D], rowf[:, R_M2:R_M2 + D], rowf[:, R_OB:R_OB + D], ALU.add
                               ).then_inc(pool_setup, 1)
            pool.wait_ge(pool_setup, 6)
            pool.tensor_copy(rowp[:, :], rowf).then_inc(pool_setup, 1)
            pool.wait_ge(pool_setup, 7)
            pool.tensor_tensor(rowf, rowf, rowp[:, :], ALU.subtract).then_inc(pool_setup, 1)
            pool.wait_ge(pool_setup, 8)
            pool.tensor_copy(rowp[QR:2 * QR, :], rowf[QR:2 * QR]).then_inc(pool_setup, 1)
            pool.wait_ge(pool_setup, 9)
            pool.tensor_copy(rowp[2 * QR:RP, :], rowf[2 * QR:RP]).then_inc(pool_setup, 1)
            pool.wait_ge(pool_setup, 10)
            pool.tensor_tensor(rowf[2 * QR:RP], rowf[2 * QR:RP], rowp[2 * QR:RP, :], ALU.subtract
                               ).then_inc(pool_setup, 1)
            pool.wait_ge(pool_setup, 11)
            pool.tensor_copy(rowp[2 * QR:RP, :], rowf[2 * QR:RP]).then_inc(pool_setup, 1)
            pool.wait_ge(pool_setup, 12)

            def norm2(b):
                pool.wait_ge(var_ready, b + 1)
                pool.tensor_tensor(ln2[:, 4, :], ln2[:, 3, :], power[:, 0:TB], ALU.pow).then_inc(rstd_ready, 1)

            def add_y(b):
                pool.wait_ge(act_y, b + 2)
                pool.wait_ge(norm1, 3)
                need(pool, rstd_ready, b)
                pool.tensor_tensor(xy[:, :], yS[:, :], xn[:, b * TB:(b + 1) * TB, :].rearrange("p t d -> p (t d)"),
                                   ALU.add).then_inc(xy_ready, 1)

            for k in range(K):
                for h in range(2):
                    first = h * T // 2
                    if k:
                        pool.wait_ge(scattered[h], 16 * T // 2)
                    pool.tensor_copy(xrow[:, first:first + T // 2, D:DR].rearrange("p t d -> p (t d)").bitcast(I32),
                                     const[:, C_ID0 + k * T + first:C_ID0 + k * T + first + T // 2]
                                     ).then_inc(row_ids, 1)
                    pool.wait_ge(row_ids, 2 * k + h + 1)
                    if k == 0 and h == 0:
                        pool.wait_ge(slots_ready, 1)
                        pool.wait_ge(xs_zero, 16)
                        pool.wait_ge(xh_ready, NB)
                    for t in range(first, first + T // 2):
                        if k == 1 and t == T - 2:
                            norm2(0)
                        pool.indirect_dma_start(xs_d, bass.IndirectOffsetOnAxis(ap=sloti[:, k, t:t + 1], axis=0),
                                                xrow[:, t, :], None).then_inc(scattered[h], 16)

            def attend(b, beside):
                for n in range(4):
                    beside(n)
                if b:
                    add_y(b)
                for n in range(4, 6):
                    beside(n)
                if b:
                    norm2(b)
                for n in range(6, STEPS):
                    beside(n)

            def take_ids(t):
                u = t[1] % RING
                pool.wait_ge(row_in[u], 16 * turn_of(t) + 16)
                need(pool, row_out[u], 16 * turn_of(t))
                pool.tensor_copy(ids[:, u:u + 1], xg[:, u, D:DR].bitcast(I32)).then_inc(pool_ids, 1)

            def scatter(t):
                u = t[1] % RING
                pool.wait_ge(dve_eo, tile(t) + 1)
                pool.wait_ge(pool_ids, tile(t) + 1)
                pool.indirect_dma_start(es_d, bass.IndirectOffsetOnAxis(ap=ids[:, u:u + 1], axis=0),
                                        eo[:, u, :], None).then_inc(row_out[u], 16)

            def step(t):
                for part, k in ((take_ids, 2), (scatter, 0)):
                    if exists(after(t, k)):
                        part(after(t, k))

            sequences(pool, attend, step, unroll=True)
            def norm3(h):
                pool.wait_ge(var3_ready, h + 1)
                pool.tensor_tensor(rstd3[:, h * T // 2:(h + 1) * T // 2], ln3[:, 3, :], power[:, :], ALU.pow
                                   ).then_inc(rstd3_ready, 1)

            for b in range(NB // 2, NB):
                pool.wait_ge(gathered[b], 16 * K)
            pool.wait_ge(gates, 3)
            for k in range(K):
                row = rowsk[:, k, T // 2:T, :]
                pool.tensor_tensor(row, row, gw[:, k, T // 2:T].unsqueeze(2).to_broadcast([P, T // 2, D]), ALU.mult
                                   ).then_inc(pool_weigh, 1)
            norm3(0)
            first = comb[:, 0:T // 2, :]
            pool.wait_ge(rstd3_ready, 1)
            pool.wait_ge(scaled3, 1)
            pool.tensor_tensor(first, first, rstd3[:, 0:T // 2].unsqueeze(2).to_broadcast([P, T // 2, D]), ALU.mult
                               ).then_inc(pool_w3, 1)
            norm3(1)
            pool.wait_ge(pool_w3, 1)
            pool.wait_ge(dve_acc, 3)
            pool.tensor_tensor(first, first, acc[:, 0:T // 2, :], ALU.add).then_inc(out0_ready, 1)

        @block.scalar
        def _(act):
            def norm(tiles):
                for t in tiles:
                    ins = act.activation(xn[:, t, :], x[:, t, :], ACT.Identity, scale=lnt[:, 5, t:t + 1],
                                         bias=lnt[:, 10, t:t + 1])
                ins.then_inc(norm1, 1)

            act.wait_ge(nmr_ready, 1)
            norm(range(T // 4))
            act.wait_ge(w_in, 64)
            def first_norm(b):
                act.activation(xa[:, :] if b == 0 else xn1T[:, b * SEQ:(b + 1) * SEQ], XT4[b][:, :], ACT.Identity,
                               scale=vec[:, V_G1:V_G1 + 1], bias=vec[:, V_B1:V_B1 + 1]
                               ).then_inc(xa_ready if b == 0 else act_xn, 1)

            for b in range(NB):
                act.wait_ge(pe_xT, b + 1)
                if b >= 2:
                    act.wait_ge(pe_logit, b - 1)
                act.activation(xrT[:, b % 2, :], XT4[b][:, :], ACT.Identity,
                               scale=vec[:, V_RW:V_RW + 1], bias=vec[:, V_RB:V_RB + 1]).then_inc(act_xT, 1)
                if b == 0:
                    first_norm(0)
            for b in range(1, NB):
                first_norm(b)
            norm(range(T // 4, T // 2))

            def start(n):
                if n == 4:
                    norm(range(T // 2, T))
                if n == 1:
                    act.wait_ge(diff_ready, 1)
                    act.activation(gw[:, 2, :], gw[:, 3, :], ACT.Exp).then_inc(diff_exp, 1)

            def warm(function, n):
                need(act, act_warm, n)
                act.activation(spare[:, :], const[:, C_ONE:C_ONE + 1], function).then_inc(act_warm, 1)

            act.sem_inc(act_gelu, FC)
            act.sem_inc(act_y, 1)
            act.wait_ge(pool_const, 3)

            def attend(b, beside):
                act.wait_ge(pe_q, b + 1)
                act.activation(qT[:, :], GA[:, :], ACT.Identity, scale=float(DH) ** -0.5).then_inc(act_q, 1)
                act.wait_ge(pe_k, b + 1)
                act.wait_ge(dve_kx, b + 1)
                need(act, act_kx, b)
                act.activation(kT[:, :], GB[:, :], ACT.Identity).then_inc(act_k, 1)
                beside(0)
                act.wait_ge(pe_drive, b + 1)
                act.wait_ge(dve_scan, b + 1)
                act.activation(drive[:, :], GC[:, :], ACT.Identity, bias=vec[:, V_BU:V_BU + 1]).then_inc(act_drive, 1)
                act.wait_ge(act_k, b + 1)
                act.wait_ge(pe_scores, NCH * b + NCH)
                mine = spread(b)[1]
                for i, (m, g) in enumerate(mine):
                    ins = act.activation(kx[:, m, g, W:], kT[:, :], ACT.Identity,
                                         scale=const[:, C_HEAD + 4 * g + m:C_HEAD + 4 * g + m + 1])
                    if i == len(mine) - 3:
                        beside(1)
                ins.then_inc(act_kx, 1)
                beside(2)
                act.wait_ge(pe_gate, b + 2)
                act.activation(gate[:, :], GB[:, :], ACT.Tanh, scale=0.5).then_inc(act_gate, 1)
                beside(3)
                warm(ACT.Exp, 2 * b)
                for c in range(NCH):
                    act.wait_ge(dve_sub, NCH * b + c + 3)
                    act.wait_ge(dve_pT, NCH * b + c + 1)
                    act.activation(pr[:, c % 2, :], sc[:, c % 2, :], ACT.Exp).then_inc(act_exp, 1)
                act.wait_ge(pe_y, b + 1)
                act.activation(yS[:, :], GA[:, :], ACT.Identity).then_inc(act_y, 1)
                warm(ACT.Gelu, 2 * b + 1)
                for n in range(4, 9):
                    beside(n)
                act.wait_ge(pe_hT, b + 1)
                act.activation(hT[:, :], GB[:, :], ACT.Identity, scale=vec[:, V_G2:V_G2 + 1],
                               bias=vec[:, V_B2:V_B2 + 1]).then_inc(act_hT, 1)
                beside(9)
                act.wait_ge(pe_mlp2, b + 1)
                for c in range(FC):
                    act.wait_ge(pe_mlp1, FC * b + c + 1)
                    act.activation(gT[:, c, :], [GA, GB, GC, GA][c][:, :], ACT.Gelu,
                                   bias=vec[:, V_M1 + c:V_M1 + c + 1]).then_inc(act_gelu, 1)
                for n in range(10, STEPS):
                    beside(n)

            def gelu(t):
                u, i = t[1] % 2, tile(t)
                act.wait_ge(pe_he, i + 1)
                need(act, pe_eo, i - 1)
                b1 = (t[1] % RING) * K_N + K_B1
                for c in range(FC):
                    ins = act.activation(heT[:, u, c * P:(c + 1) * P], S[u][:, c * P:(c + 1) * P], ACT.Gelu,
                                         bias=pk[:, b1 + c:b1 + c + 1])
                ins.then_inc(act_he, 1)

            def rows_T(t):
                i, u, w = tile(t), t[1] % 2, (t[1] % RING) * K_N
                act.wait_ge(pe_xeT, i + 1)
                act.wait_ge(pk_in[t[1] % RING], 16 * turn_of(t) + 16)
                need(act, pe_he, i - 1)
                act.activation(xeT[:, u, :], XT[:, 0:P], ACT.Identity, scale=pk[:, w + K_EW:w + K_EW + 1],
                               bias=pk[:, w + K_EB:w + K_EB + 1]).then_inc(act_xeT, 1)

            def step(t):
                for part, k in ((rows_T, 2), (gelu, 1)):
                    if exists(after(t, k)):
                        part(after(t, k))

            def end(n):
                if n == 5:
                    act.wait_ge(gates, 3)
                    for b in range(NB // 2):
                        act.wait_ge(gathered[b], 16 * K)
                        for t in range(b * TB, (b + 1) * TB):
                            act.activation(comb[:, t, :], rowsk[:, 0, t, :], ACT.Identity, scale=gw[:, 0, t:t + 1])
                            ins = act.activation(rowsk[:, 1, t, :], rowsk[:, 1, t, :], ACT.Identity,
                                                 scale=gw[:, 1, t:t + 1])
                        ins.then_inc(act_weigh, 1)

            sequences(act, attend, step, start=start, end=end)
        @block.tensor
        def _(pe):
            pe.wait_ge(w_in, 64)
            pe.wait_ge(rw_set, 1)

            def turn(b):
                pe.wait_ge(xh_ready, b + 1)
                for t in range(TB):
                    last = nc.tensor.transpose(XT4[b][:, t * P:(t + 1) * P],
                                               xhat[:, b * TB + t, :], ident)
                last.then_inc(pe_xT, 1)

            def route(b):
                pe.wait_ge(act_xT, b + 1)
                for q in range(4):
                    last = mm(GC[q * W:(q + 1) * W, b * P:(b + 1) * P], rw[:, :],
                              xrT[:, b % 2, :].rearrange("p (t q j) -> p t q j", q=4, j=W)[:, :, q, :],
                              start=True, stop=True)
                last.then_inc(pe_logit, 1)

            turn(0)
            for b in range(NB):
                if b + 1 < NB:
                    turn(b + 1)
                route(b)

            def start(n):
                if n == 0:
                    pe.wait_ge(picks_ready, 1)
                    pe.wait_ge(pool_const, 3)
                    mm(XT[:, 0:ET], const[:, C_TRI:C_TRI + P], picks, start=True, stop=True)
                    mm(EO[:, 0:ET], ones[:, :], picks, start=True, stop=True).then_inc(pe_rank, 1)

            pe.sem_inc(pe_scores, NCH)
            pe.sem_inc(pe_gate, 1)
            pe.sem_inc(pe_pv, 1)
            pe.sem_inc(pe_mlp2, 1)
            pe.wait_ge(pool_setup, 5)
            pe.wait_ge(act_xn, 1)
            pe.wait_ge(logit_read, 1)

            def bias_row(out, at):
                mm(out, sel0[:, :], rowp[:, at:at + D].unsqueeze(1).to_broadcast([RP, TB, D]),
                   start=True, stop=False, skip_group_check=True)

            def sums(out, h):
                q, k = slice(h * SEQ // 2, (h + 1) * SEQ // 2), slice(h * NBLK // 2, (h + 1) * NBLK // 2)
                for s in range(2):
                    for g in range(HG):
                        last = mm(out[g * W:(g + 1) * W, q], const[:, C_BLK:C_BLK + W], pT[:, k, g, s, :],
                                  start=(s == 0), stop=(s == 1), skip_group_check=True)
                last.then_inc(pe_den, 1)

            def per_tile(out, lhs, rhs, h=None):
                for t in range(TB) if h is None else range(h * TB // 2, (h + 1) * TB // 2):
                    last = mm(out[:, t * P:(t + 1) * P], lhs[:, t * P:(t + 1) * P], rhs, start=False,
                              stop=(t == TB - 1), skip_group_check=True)
                return last

            def pv(kb, first):
                n = 2 if kb + 1 < NBLK else 1
                lo = pT[:, kb, 0, 1, :]
                for g in range(HG):
                    rhs = bass.AP(lo.tensor, lo.offset + g * 2 * W, [list(lo.ap[0]), [HG * 2 * W - W, n], [1, W]])
                    last = mm(OV[g * W:(g + 1) * W, kb * W:(kb + n) * W], vx[:, kb, g * W:(g + 1) * W], rhs,
                              start=first, stop=(kb == NBLK - 1), skip_group_check=True)
                return last

            def attend(b, beside):
                pe.wait_ge(xa_ready, b + 1)
                pe.wait_ge(act_gelu, FC * b + 4)
                mm(GA[:, :], wqkv[:, 0:D], xa[:, :], start=True, stop=True).then_inc(pe_q, 1)
                mm(GB[:, :], wqkv[:, D:2 * D], xa[:, :], start=True, stop=True).then_inc(pe_k, 1)
                beside(0)
                mm(GC[:, :], wdrive[:, :], xa[:, :], start=True, stop=True).then_inc(pe_drive, 1)
                pe.wait_ge(act_q, b + 1)
                mm(GA[:, :], wv[:, :], xa[:, :], start=True, stop=True).then_inc(pe_v, 1)
                pe.wait_ge(act_k, b + 1)
                pe.wait_ge(pool_setup, 12)
                bias_row(GB[:, :], R_G)
                per_tile(GB, xa, wug[:, D:2 * D]).then_inc(pe_gate, 1)
                for n in range(1, 4):
                    beside(n)

                pe.wait_ge(dve_kx, b + 2)
                pe.wait_ge(act_kx, b + 1)
                if isinstance(b, int) and b == 0:
                    pe.wait_ge(act_xn, NB - 1)
                    pe.wait_ge(wo_in, 16 * 5)
                else:
                    pe.wait_ge(act_he, min(NT, NT - DRAIN + before(4) + 1) if isinstance(b, int) else (b - 1) * STEPS + LEAD - 2 + 5)
                for c in range(NCH + 3):
                    if c < NCH:
                        pe.wait_ge(dve_sub, NCH * b + c + 1)
                        m0 = maskb[:, 0:4 * W].rearrange("p (a k) -> p a k", a=2).unsqueeze(2).to_broadcast([P, 2, HG, 2 * W]) \
                            if c == 0 else maskb[:, 2 * W:4 * W].unsqueeze(1).to_broadcast([P, 2 * HG, 2 * W])
                        mm(S[c % 2][:, :], identb[:, :], m0, start=True, stop=False, skip_group_check=True)
                        for k in range(2):
                            j = 2 * c + k
                            for m in range(4):
                                last = mm(S[c % 2][m * W:(m + 1) * W, k * 256:(k + 1) * 256],
                                          qT[:, j * W:(j + 1) * W], kx[:, m, :, j * W:(j + 2) * W],
                                          start=False, stop=(k == 1), skip_group_check=True)
                        last.then_inc(pe_scores, 1)
                    if c == 3:
                        pe.wait_ge(dve_scan, b + 2)
                        pe.wait_ge(dve_vx, b + 1)
                        for t in range(TB):
                            last = mm(GA[:, t * P:(t + 1) * P], states[:, t * P:(t + 1) * P], cw[:, :],
                                      start=True, stop=True)
                        last.then_inc(pe_y, 1)
                        pe.wait_ge(dve_acc, b + 1)
                    if c >= 3:
                        n = c - 3
                        pe.wait_ge(dve_pT, NCH * b + n + 3)
                        if n:
                            pv(2 * n - 1, False)
                        last = pv(2 * n, n == 0)
                        if n == NCH - 3:
                            pe.wait_ge(act_drive, b + 1)
                            sums(GC, 0)
                last = pv(NBLK - 1, False)
                last.then_inc(pe_pv, 1)
                pe.wait_ge(act_gate, b + 1)
                sums(GB, 1)
                pe.wait_ge(dve_sub, NCH * b + NCH + 2)
                beside(4)
                pe.wait_ge(dve_rden, 2 * b + 1)
                bias_row(GC[:, :], R_O)
                for h in range(2):
                    pe.wait_ge(dve_oT, 2 * b + h + 1)
                    last = per_tile(GC, oT, wo[:, :], h)
                last.then_inc(pe_attn, 1)
                for n in range(5, 9):
                    beside(n)
                pe.wait_ge(dve_h, b + 1)
                for t in range(TB):
                    last = nc.tensor.transpose(GB[:, t * P:(t + 1) * P], hh[:, t * P:(t + 1) * P], ident)
                last.then_inc(pe_hT, 1)
                beside(9)
                pe.wait_ge(act_hT, b + 1)
                for c in range(FC):
                    if c == 0:
                        pe.wait_ge(act_y, b + 2)
                    if c == 2:
                        pe.wait_ge(dve_attn, b + 1)
                    if c == 3:
                        pe.wait_ge(act_gelu, FC * b + 5)
                    mm([GA, GB, GC, GA][c][:, :], m1[:, c * P:(c + 1) * P], hT[:, :], start=True, stop=True
                       ).then_inc(pe_mlp1, 1)
                beside(10)
                bias_row(OV[:, :], R_M2)
                for c in range(FC):
                    pe.wait_ge(act_gelu, FC * b + c + 5)
                    for t in range(TB):
                        last = mm(OV[:, t * P:(t + 1) * P], gT[:, c, t * P:(t + 1) * P], m2[:, c, :],
                                  start=False, stop=(c == FC - 1), skip_group_check=True)
                last.then_inc(pe_mlp2, 1)
                for n in range(11, STEPS):
                    beside(n)

            def rows_T(t):
                i, u = tile(t), t[1] % RING
                pe.wait_ge(row_in[u], 16 * turn_of(t) + 16)
                need(pe, act_xeT, i)
                nc.tensor.transpose(XT[:, 0:P], xg[:, u, 0:D], ident).then_inc(pe_xeT, 1)

            def layer1(t):
                i, u, w = tile(t), t[1] % 2, (t[1] % RING) * K_N + K_W1
                pe.wait_ge(act_xeT, i + 1)
                pe.wait_ge(pk_in[t[1] % RING], 16 * turn_of(t) + 16)
                need(pe, act_he, i - 1)
                for c in range(FC):
                    last = mm(S[u][:, c * P:(c + 1) * P], pk[:, w + c * P:w + (c + 1) * P], xeT[:, u, :],
                              start=True, stop=True)
                last.then_inc(pe_he, 1)

            def layer2(t):
                i, u, w = tile(t), t[1] % 2, (t[1] % RING) * K_N + K_W2
                pe.wait_ge(act_he, i + 1)
                need(pe, dve_eo, i)
                for c in range(FC):
                    last = mm(EO[:, 0:P], heT[:, u, c * P:(c + 1) * P], pk[:, w + c * P:w + (c + 1) * P],
                              start=(c == 0), stop=(c == FC - 1))
                last.then_inc(pe_eo, 1)

            def step(t):
                for part, k in ((rows_T, 2), (layer1, 1), (layer2, 0)):
                    if exists(after(t, k)):
                        part(after(t, k))

            sequences(pe, attend, step, start=start)

        @block.vector
        def _(v):
            count = [0]
            link = chain(v, count)
            tt, ts, stt = v.tensor_tensor, v.tensor_scalar, v.scalar_tensor_tensor

            def moments(stats, out, done=dve):
                me, ve, mo, vo = (stats[:, :, n] for n in (1, 2, 4, 5))
                tt(out[:, 0, :], me, mo, ALU.add).then_inc(done, 1)
                tt(out[:, 1, :], me, mo, ALU.subtract).then_inc(done, 1)
                tt(out[:, 2, :], ve, vo, ALU.add).then_inc(done, 1)
                return 3

            v.sem_inc(dve_sub, 2)
            v.sem_inc(dve_pT, 2)
            v.sem_inc(dve_kx, 1)
            v.sem_inc(dve_scan, 1)
            v.sem_inc(dve_acc, 1)

            for b in range(NB):
                v.wait_ge(x_in[b], 16)
                for t in range(b * TB, b * TB + TB):
                    ins = v.bn_stats(st[:, t, :], x[:, t, :])
            link(ins)
            count[0] += moments(st, lnt)
            v.wait_ge(dve, count[0])
            ts(lnt[:, 0, :], lnt[:, 0, :], 0.5, None, ALU.mult).then_inc(dve, 1)
            count[0] += 1
            link(tt(lnt[:, 1, :], lnt[:, 1, :], lnt[:, 1, :], ALU.mult))
            link(stt(lnt[:, 2, :], lnt[:, 1, :], D / 4, lnt[:, 2, :], ALU.mult, ALU.add))
            link(ts(lnt[:, 3, :], lnt[:, 2, :], 1.0 / D, EPS, ALU.mult, ALU.add))
            link(v.reciprocal(lnt[:, 1, :], lnt[:, 3, :]))
            link(stt(lnt[:, 2, :], lnt[:, 2, :], 1.0 / D, lnt[:, 1, :], ALU.mult, ALU.mult))
            link(ts(lnt[:, 4, :], lnt[:, 2, :], EPS, None, ALU.add))
            a, y, w = lnt[:, 3:5, :], lnt[:, 5:7, :], lnt[:, 8:10, :]
            link(ts(w.bitcast(I32), a.bitcast(I32), 1, None, ALU.logical_shift_right))
            link(ts(y.bitcast(I32), w.bitcast(I32), -1.0, float(MAGIC), ALU.mult, ALU.add))
            for _ in range(3):
                link(tt(w, y, y, ALU.mult))
                link(stt(w, w, -0.5, a, ALU.mult, ALU.mult))
                link(stt(y, w, 1.5, y, ALU.add, ALU.mult))
            tt(lnt[:, 7, :], lnt[:, 5, :], lnt[:, 6, :], ALU.mult).then_inc(dve, 1)
            count[0] += 1
            stt(lnt[:, 10, :], lnt[:, 0, :], -1.0, lnt[:, 5, :], ALU.mult, ALU.mult).then_inc(nmr_ready, 1)
            v.wait_ge(dve, count[0])

            for b in range(NB):
                for t in range(TB * b, TB * b + TB):
                    ins = ts(xhat[:, t, :], x[:, t, :], lnt[:, 0, t:t + 1], lnt[:, 7, t:t + 1], ALU.subtract, ALU.mult)
                ins.then_inc(xh_ready, 1)

            v.wait_ge(w_in, 64)
            v.wait_ge(pe_logit, NB)
            link(v.transpose(logitq, GC[:, :]))
            link(tt(logit[:, :, :], logitq.rearrange("p (t e) -> p t e", e=W)[:, :, 0:E],
                    rb[:, :].unsqueeze(1).to_broadcast([P, T, E]), ALU.add))
            v.sem_inc(logit_read, 1)
            for t in range(T):
                ins = v.max(top[:, t, :], logit[:, t, :])
            link(ins)
            for t in range(T):
                ins = v.max_index(topi[:, t, :], top[:, t, :], logit[:, t, :])
            link(ins)
            link(v.tensor_copy(topf[:, :, :].rearrange("p k t -> p t k"), topi[:, :, 0:K]))
            for k in range(K):
                ins = tt(pick[:, k, :, :], topf[:, k, :].unsqueeze(1).to_broadcast([P, E, T]),
                         const[:, C_IE:C_IE + E].unsqueeze(2).to_broadcast([P, E, T]), ALU.is_equal)
            link(ins)
            tt(picks[:, :].rearrange("p (e t) -> p e t", e=E), pick[:, 0, :, :], pick[:, 1, :, :], ALU.add
               ).then_inc(picks_ready, 1)
            tt(gw[:, 3, :], top[:, :, 1], top[:, :, 0], ALU.subtract).then_inc(diff_ready, 1)
            v.wait_ge(pe_rank, 1)
            link(v.tensor_copy(tot[:, :], EO[:, 0:E * T]))
            link(v.tensor_tensor_scan(incl[:, :], const[:, C_RESET:C_RESET + E * T], tot[:, :], 0.0, ALU.mult, ALU.add))
            incl3 = incl[:, :].rearrange("p (e t) -> p e t", e=E)
            link(tt(cmpj[:, :, :], incl3[:, :, T - 1:T].to_broadcast([P, E, MB]),
                    const[:, C_J:C_J + MB].unsqueeze(1).to_broadcast([P, E, MB]), ALU.is_gt))
            link(v.tensor_reduce(blocks[:, 0, :], cmpj[:, :, :], AX_X, ALU.add))
            link(v.tensor_tensor_scan(blocks[:, 1, :], const[:, C_ONE:C_ONE + E], blocks[:, 0, :], 0.0, ALU.mult, ALU.add))
            link(tt(blocks[:, 2, :], blocks[:, 1, :], blocks[:, 0, :], ALU.subtract))
            link(ts(blocks[:, 3, :], blocks[:, 2, :], float(P), None, ALU.mult))
            link(tt(base[:, :], incl[:, :], tot[:, :], ALU.subtract))
            link(tt(base[:, :], base[:, :], XT[:, 0:E * T], ALU.add))
            link(tt(base[:, :].rearrange("p (e t) -> p e t", e=E), base[:, :].rearrange("p (e t) -> p e t", e=E),
                    blocks[:, 3, :].unsqueeze(2).to_broadcast([P, E, T]), ALU.add))
            for k in range(K):
                ins = tt(slotf[:, k, :, :], pick[:, k, :, :], base[:, :].rearrange("p (e t) -> p e t", e=E), ALU.mult)
            link(ins)
            for k in range(K):
                ins = v.tensor_reduce(slots[:, k, :], slotf[:, k, :, :].rearrange("p e t -> p t e"), AX_X, ALU.add)
            link(ins)
            v.tensor_copy(sloti[:, :, :], slots[:, :, :]).then_inc(slots_ready, 1)

            link(tt(tcmp[:, :, :], const[0:1, C_TI:C_TI + NT].unsqueeze(2).to_broadcast([1, NT, E]),
                    blocks[0:1, 1, :].unsqueeze(1).to_broadcast([1, NT, E]), ALU.is_ge))
            link(v.tensor_reduce(texpf[:, 0, :], tcmp[:, :, :], AX_X, ALU.add))
            link(ts(texpf[:, 1, :], texpf[:, 0, :], float(E - 1), None, ALU.min))
            v.tensor_copy(texp[:, :], texpf[:, 1, :]).then_inc(texp_ready, 1)

            def start(n):
                if n == 8:
                    v.wait_ge(diff_exp, 1)
                    ts(gw[:, 3, :], gw[:, 2, :], 1.0, None, ALU.add).then_inc(gates, 1)
                    v.wait_ge(gates, 1)
                    v.reciprocal(gw[:, 0, :], gw[:, 3, :]).then_inc(gates, 1)
                    v.wait_ge(gates, 2)
                    tt(gw[:, 1, :], gw[:, 2, :], gw[:, 0, :], ALU.mult).then_inc(gates, 1)

            CH = 11
            k0 = count[0]

            def attend(b, beside):
                n = [0]

                def link1(ins):
                    n[0] += 1
                    ins.then_inc(dve, 1)
                    v.wait_ge(dve, b * CH + k0 + n[0])

                v.wait_ge(act_k, b + 1)
                v.wait_ge(pe_scores, NCH * b + NCH)
                beside(0)
                for i, (m, g) in enumerate(spread(b)[0]):
                    if i == 8:
                        beside(1)
                    ins = ts(kx[:, m, g, W:], kT[:, :], const[:, C_HEAD + 4 * g + m:C_HEAD + 4 * g + m + 1],
                             None, ALU.mult)
                ins.then_inc(dve_kx, 1)
                beside(2)
                v.wait_ge(pe_pv, b + 1)
                v.wait_ge(pe_v, b + 1)
                link1(v.transpose(vT[:, :], GA[:, :]))
                tt(vx[:, :, :].rearrange("p k (g m d) -> p (k g) m d", g=HG, m=4),
                   vT[:, :].rearrange("p (n d) -> p n d", d=DH).unsqueeze(2).to_broadcast([P, NBLK * HG, 4, DH]),
                   const[:, C_BLK:C_BLK + W].rearrange("p (m d) -> p m d", m=4).unsqueeze(1).to_broadcast(
                       [P, NBLK * HG, 4, DH]), ALU.mult).then_inc(dve_vx, 1)
                beside(3)
                v.wait_ge(act_drive, b + 1)
                v.tensor_tensor_scan(states[:, :], vec[:, V_A:V_A + 1].to_broadcast([P, SEQ]), drive[:, :], 0.0,
                                     ALU.mult, ALU.add).then_inc(dve_scan, 1)
                for c in range(NCH + 1):
                    if c < NCH:
                        s3 = S[c % 2][:, :].rearrange("p (u k) -> p u k", u=8)
                        v.wait_ge(pe_scores, NCH * b + NCH + c + 1)
                        v.tensor_reduce(smax[:, c % 2, :], s3, AX_X, ALU.max).then_inc(dve_max, 1)
                        v.wait_ge(dve_max, NCH * b + c + 1)
                        if c >= 2:
                            v.wait_ge(act_exp, NCH * b + c - 1)
                        tt(sc[:, c % 2, :].rearrange("p (u k) -> p u k", u=8), s3,
                           smax[:, c % 2, :].unsqueeze(2).to_broadcast([P, 8, 2 * W]), ALU.subtract
                           ).then_inc(dve_sub, 1)
                    if c >= 1:
                        i = c - 1
                        v.wait_ge(act_exp, NCH * b + i + 1)
                        v.transpose(pT[:, 2 * i:2 * i + 2, :, :, :].rearrange("p a g s q -> p (a g s q)"),
                                    pr[:, i % 2, :]).then_inc(dve_pT, 1)
                for h in range(2):
                    q = slice(h * SEQ // 2, (h + 1) * SEQ // 2)
                    v.wait_ge(pe_den, 2 * b + h + 1)
                    v.reciprocal(rden[:, q], [GC, GB][h][:, q]).then_inc(dve_rden, 1)
                    v.wait_ge(dve_rden, 2 * b + h + 1)
                    v.wait_ge(pe_pv, b + 2)
                    tt(oT[:, q], OV[:, q], rden[:, q], ALU.mult).then_inc(dve_oT, 1)
                beside(4)
                v.wait_ge(act_y, b + 2)
                if isinstance(b, int) and b == 0:
                    v.wait_ge(norm1, 3)
                    tt(xy[:, :], yS[:, :], xn[:, 0:TB, :].rearrange("p t d -> p (t d)"), ALU.add
                       ).then_inc(xy_ready, 1)
                v.wait_ge(pe_attn, b + 1)
                tt(mix[:, 1, :], GC[:, :], yS[:, :], ALU.subtract).then_inc(dve_attn, 1)
                v.wait_ge(dve_attn, b + 1)
                v.wait_ge(act_gate, b + 1)
                link1(stt(mix[:, 2, :], gate[:, :], 1.0, mix[:, 1, :], ALU.add, ALU.mult))
                v.wait_ge(xy_ready, b + 1)
                link1(stt(x2[:, :], mix[:, 2, :], 0.5, xy[:, :], ALU.mult, ALU.add))
                beside(5)
                for t in range(TB):
                    ins = v.bn_stats(st2[:, t, :], x2[:, t * D:(t + 1) * D])
                link1(ins)
                n[0] += moments(st2, ln2)
                v.wait_ge(dve, b * CH + k0 + n[0])
                link1(ts(ln2[:, 0, :], ln2[:, 0, :], 0.5, None, ALU.mult))
                link1(tt(ln2[:, 1, :], ln2[:, 1, :], ln2[:, 1, :], ALU.mult))
                link1(stt(ln2[:, 2, :], ln2[:, 1, :], D / 4, ln2[:, 2, :], ALU.mult, ALU.add))
                ts(ln2[:, 3, :], ln2[:, 2, :], 1.0 / D, EPS, ALU.mult, ALU.add).then_inc(var_ready, 1)
                if not (isinstance(b, int) and b == NB - 1):
                    v.wait_ge(pe_gate, b + 2)
                    v.tensor_copy(xa[:, :], xn1T[:, bass.ds((b + 1) * SEQ, SEQ)]).then_inc(xa_ready, 1)
                beside(6)
                v.wait_ge(rstd_ready, b + 1)
                for t in range(TB):
                    ins = ts(hh[:, t * D:(t + 1) * D], x2[:, t * D:(t + 1) * D], ln2[:, 0, t:t + 1],
                             ln2[:, 4, t:t + 1], ALU.subtract, ALU.mult)
                ins.then_inc(dve_h, 1)
                beside(7)
                link1(tt(mix[:, 0, :], x2[:, :], x[:, bass.ds(b * TB, TB), :].rearrange("p t d -> p (t d)"), ALU.add))
                for k in range(8, 11):
                    beside(k)
                v.wait_ge(pe_mlp2, b + 2)
                for h in range(2):
                    v.wait_ge(scattered[h], 16 * K * T // 2)
                tt(acc[:, bass.ds(b * TB, TB), :], tok3(OV[:, :]), tok3(mix[:, 0, :]), ALU.add
                   ).then_inc(dve_acc, 1)
                for k in range(11, STEPS):
                    beside(k)
                assert n[0] == CH, n[0]

            def finish(t):
                i, u, w = tile(t), t[1] % RING, (t[1] % RING) * K_N + K_B2
                v.wait_ge(pe_eo, i + 1)
                need(v, row_out[u], 16 * turn_of(t))
                tt(eo[:, u, :], EO[:, 0:P], pk[:, w:w + D], ALU.add).then_inc(dve_eo, 1)

            def step(t):
                if exists(t):
                    finish(t)

            HT2 = T // 2

            def combine(h):
                n = [h * 8]
                tiles = range(h * HT2, (h + 1) * HT2)

                def link3(ins):
                    n[0] += 1
                    ins.then_inc(comb_chain, 1)
                    v.wait_ge(comb_chain, n[0])

                v.wait_ge(*((act_weigh, 2), (pool_weigh, 2))[h])
                own = slice(h * HT2, (h + 1) * HT2)
                link3(tt(comb[:, own, :], (comb[:, own, :], rowsk[:, 0, own, :])[h], rowsk[:, 1, own, :], ALU.add))
                for t in tiles:
                    ins = v.bn_stats(st3[:, t % HT2, :], comb[:, t, :])
                link3(ins)
                moments(st3, ln3, comb_chain)
                n[0] += 3
                v.wait_ge(comb_chain, n[0])
                link3(ts(ln3[:, 0, :], ln3[:, 0, :], 0.5, None, ALU.mult))
                link3(tt(ln3[:, 1, :], ln3[:, 1, :], ln3[:, 1, :], ALU.mult))
                link3(stt(ln3[:, 2, :], ln3[:, 1, :], D / 4, ln3[:, 2, :], ALU.mult, ALU.add))
                if h:
                    v.wait_ge(rstd3_ready, 1)
                ts(ln3[:, 3, :], ln3[:, 2, :], 1.0 / D, EPS, ALU.mult, ALU.add).then_inc(var3_ready, 1)
                for t in tiles:
                    ins = stt(comb[:, t, :], comb[:, t, :], ln3[:, 0, t % HT2:t % HT2 + 1], ow[:, :],
                              ALU.subtract, ALU.mult)
                ins.then_inc(scaled3, 1)
                v.wait_ge(scaled3, h + 1)

            def out(b):
                v.wait_ge(rstd3_ready, 2)
                v.wait_ge(dve_acc, b + 2)
                for t in range(b * TB, b * TB + TB):
                    ins = stt(comb[:, t, :], comb[:, t, :], rstd3[:, t:t + 1], acc[:, t, :], ALU.mult, ALU.add)
                ins.then_inc(out_ready, 1)

            def end(n):
                if n == 8:
                    combine(0)
                if n == 10:
                    combine(1)
                    out(2)

            sequences(v, attend, step, start=start, end=end)
            out(3)


def kernel(**inputs):
    import concourse.bacc as _bacc
    from concourse.bass_utils import run_bass_kernel_spmd as _run

    a = {k: np.ascontiguousarray(v) for k, v in inputs.items()}

    def at(n):
        return a["L0_attn_" + n]

    def ft(n):
        return a["L0_ffn_" + n]

    bug = at("b_ug")
    vec = np.concatenate(
        [np.stack([at("ln1_g"), at("ln1_b"), at("ln2_g"), at("ln2_b"), bug[:D], at("A"), ft("router_ln_w"),
                   ft("router_ln_b")]), at("mlp_b1").reshape(FC, P)]).T
    row = np.zeros((3, QR, R_N), np.float32)
    for at_, n in ((R_G, bug[D:]), (R_O, at("b_O")), (R_M2, at("mlp_b2")), (R_OB, ft("out_ln_b"))):
        row[:, 0, at_:at_ + D] = n
    pk = np.concatenate(
        [ft("w1"), ft("w2").reshape(E, FC, P, D).transpose(0, 2, 1, 3).reshape(E, P, FC * D),
         ft("exp_ln_w")[:, :, None], ft("exp_ln_b")[:, :, None], ft("b1").reshape(E, FC, P).transpose(0, 2, 1),
         np.broadcast_to(ft("b2")[:, None, :], (E, P, D))], axis=2)
    arrays = {
        "x": at("x"), "const": constants(), "vec": np.ascontiguousarray(vec), "row": row.reshape(RP, R_N),
        "wqkv": at("W_qkv"), "wo": at("W_O"), "wug": at("W_ug"), "bw": at("B_w"), "cw": at("C_w"),
        "m1": at("mlp_W1"), "m2": at("mlp_W2"), "rw": ft("router_w"), "rb": ft("router_b"), "pk": np.ascontiguousarray(pk),
        "ow": ft("out_ln_w"),
    }
    nc = _bacc.Bacc("TRN2", target_bir_lowering=False, num_devices=1)
    args = [nc.dram_tensor(f"in_{n}", v.shape, mybir.dt.from_np(v.dtype), kind="ExternalInput").ap()
            for n, v in arrays.items()]
    out = nc.dram_tensor("out_0", (NB, SEQ, D), F32, kind="ExternalOutput").ap()
    program(nc, *args, out)
    r = _run(nc, [{f"in_{n}": v for n, v in arrays.items()}], core_ids=[0])
    return r.results[0]["out_0"]
```
